# Optimizing a Trainium2 kernel written in Bass

```python
import numpy as np
import jax
import jax.numpy as jnp

def _softmax(x, axis=-1):
    return jax.nn.softmax(x, axis=axis)

def _gelu(x):
    return jax.nn.gelu(x, approximate=True)

def _silu(x):
    return jax.nn.silu(x)

def _sigmoid(x):
    return jax.nn.sigmoid(x)

def _layernorm(x, axis=-1, eps=1e-05):
    m = jnp.mean(x, axis=axis, keepdims=True)
    v = jnp.var(x, axis=axis, keepdims=True)
    return (x - m) / jnp.sqrt(v + eps)

def _scatter_add(tgt, idx, src, axis=0):
    return tgt.at[idx].add(src)

def _segment_sum(src, seg, n):
    return jax.ops.segment_sum(src, seg, n)
kernel_name = 'mk_prb_d1_jaxref_r8_c8433b'

def setup_inputs(seed: int=0):
    np.random.seed(seed)
    _w = jnp.asarray

    def _L0_attn_setup():
        import jax, jax.numpy as jnp
        import numpy as np
        import math
        B, SEQ, DIM, HEADS = (1, 256, 256, 8)
        L_INIT = 0.8 - 0.6 * math.exp(-0.3 * 1)
        EPS = 1e-06
        key = jax.random.key(seed)
        ks = jax.random.split(key, 9)
        x = jax.random.normal(ks[0], (B, SEQ, DIM), jnp.float32)
        l_q1 = jax.random.normal(ks[1], (HEADS,), jnp.float32) * 0.1
        l_k1 = jax.random.normal(ks[2], (HEADS,), jnp.float32) * 0.1
        l_q2 = jax.random.normal(ks[3], (HEADS,), jnp.float32) * 0.1
        l_k2 = jax.random.normal(ks[4], (HEADS,), jnp.float32) * 0.1
        s = 1.0 / math.sqrt(DIM)
        wq = jax.random.normal(ks[5], (2 * DIM, DIM), jnp.float32) * s
        wk = jax.random.normal(ks[6], (2 * DIM, DIM), jnp.float32) * s
        wv = jax.random.normal(ks[7], (DIM, DIM), jnp.float32) * s
        wo = jax.random.normal(ks[8], (DIM, DIM), jnp.float32) * s
        return {'x': x, 'l_q1': l_q1, 'l_k1': l_k1, 'l_q2': l_q2, 'l_k2': l_k2, 'wq': wq, 'wk': wk, 'wv': wv, 'wo': wo}
    _L0_attn_in = _L0_attn_setup()

    def _L0_ffn_setup():
        import jax, jax.numpy as jnp
        import numpy as np
        TOP_K = 4
        key = jax.random.key(seed)
        ks = jax.random.split(key, 8)
        B, S, D, E, H, HS = (2, 256, 256, 16, 128, 512)
        scaled = lambda k, shape, fan: jax.random.normal(k, shape, jnp.float32) * fan ** (-0.5)
        return {'x': jax.random.normal(ks[0], (B, S, D), jnp.float32), 'w_router': scaled(ks[1], (D, E), D), 'we1': scaled(ks[2], (E, D, H), D), 'we3': scaled(ks[3], (E, D, H), D), 'we2': scaled(ks[4], (E, H, D), H), 'ws1': scaled(ks[5], (D, HS), D), 'ws3': scaled(ks[6], (D, HS), D), 'ws2': scaled(ks[7], (HS, D), HS)}
    _L0_ffn_in = _L0_ffn_setup()
    _d = {'L0_attn_x': _L0_attn_in['x'], 'L0_attn_l_q1': _L0_attn_in['l_q1'], 'L0_attn_l_k1': _L0_attn_in['l_k1'], 'L0_attn_l_q2': _L0_attn_in['l_q2'], 'L0_attn_l_k2': _L0_attn_in['l_k2'], 'L0_attn_wq': _L0_attn_in['wq'], 'L0_attn_wk': _L0_attn_in['wk'], 'L0_attn_wv': _L0_attn_in['wv'], 'L0_attn_wo': _L0_attn_in['wo'], 'L0_ffn_w_router': _L0_ffn_in['w_router'], 'L0_ffn_we1': _L0_ffn_in['we1'], 'L0_ffn_we3': _L0_ffn_in['we3'], 'L0_ffn_we2': _L0_ffn_in['we2'], 'L0_ffn_ws1': _L0_ffn_in['ws1'], 'L0_ffn_ws3': _L0_ffn_in['ws3'], 'L0_ffn_ws2': _L0_ffn_in['ws2']}
    _x0 = _d['L0_attn_x']
    _d['L0_attn_x'] = jax.random.normal(jax.random.fold_in(jax.random.key(seed), 1), (4, 1024, 256), dtype=_x0.dtype)
    del _x0
    return _d

def reference(L0_attn_x, L0_attn_l_q1, L0_attn_l_k1, L0_attn_l_q2, L0_attn_l_k2, L0_attn_wq, L0_attn_wk, L0_attn_wv, L0_attn_wo, L0_ffn_w_router, L0_ffn_we1, L0_ffn_we3, L0_ffn_we2, L0_ffn_ws1, L0_ffn_ws3, L0_ffn_ws2):

    def _L0_attn_ref(x, l_q1, l_k1, l_q2, l_k2, wq, wk, wv, wo):
        import jax, jax.numpy as jnp
        import numpy as np
        import math
        B, SEQ, DIM, HEADS = (1, 256, 256, 8)
        L_INIT = 0.8 - 0.6 * math.exp(-0.3 * 1)
        EPS = 1e-06
        b, s, d = x.shape
        nh = HEADS
        lmbda = jnp.exp(jnp.sum(l_q1 * l_k1)) - jnp.exp(jnp.sum(l_q2 * l_k2)) + L_INIT
        q = jnp.einsum('bsd,od->bso', x, wq)
        k = jnp.einsum('bsd,od->bso', x, wk)
        v = jnp.einsum('bsd,od->bso', x, wv)

        def split_heads(t):
            return t.reshape(b, s, nh, -1).transpose(0, 2, 1, 3)
        q, k, v = map(split_heads, (q, k, v))

        def prep(t):
            dh = t.shape[-1] // 2
            t = t.reshape(b, nh, s, 2, dh)
            return t.transpose(0, 1, 3, 2, 4).reshape(b, nh * 2, s, dh)
        q, k = (prep(q), prep(k))
        dh = q.shape[-1]
        scores = jnp.einsum('bhqd,bhkd->bhqk', q, k) / math.sqrt(dh)
        causal = jnp.triu(jnp.full((s, s), -jnp.inf, dtype=scores.dtype), 1)
        attn = jax.nn.softmax((scores + causal[None, None]).astype(jnp.float32), axis=-1).astype(scores.dtype)
        attn = attn[:, :nh] - attn[:, nh:] * lmbda
        out = jnp.einsum('bhqk,bhkd->bhqd', attn, v)
        dv = out.shape[-1]
        o = out.reshape(b, nh, s, nh, dv // nh)
        o32 = o.astype(jnp.float32)
        o = (o32 * jax.lax.rsqrt(jnp.mean(o32 * o32, axis=-1, keepdims=True) + EPS)).astype(o.dtype)
        o = o.reshape(b, nh, s, dv) * (1.0 - L_INIT)
        o = o.transpose(0, 2, 1, 3).reshape(b, s, nh * dv)
        return jnp.einsum('bsd,od->bso', o, wo)

    def _L0_ffn_ref(x, w_router, we1, we3, we2, ws1, ws3, ws2):
        import jax, jax.numpy as jnp
        import numpy as np
        TOP_K = 4
        B, S, D = x.shape
        T = B * S
        E = w_router.shape[1]
        xt = x.reshape(T, D)
        probs = jax.nn.softmax(xt @ w_router, axis=-1)
        top_w, top_i = jax.lax.top_k(probs, TOP_K)
        top_w = top_w / jnp.sum(top_w, axis=-1, keepdims=True)
        cw = jnp.zeros((T, E), xt.dtype).at[jnp.arange(T)[:, None], top_i].add(top_w)
        g = jax.nn.silu(jnp.einsum('td,edh->teh', xt, we1)) * jnp.einsum('td,edh->teh', xt, we3)
        g = g * cw[:, :, None]
        moe_out = jnp.einsum('teh,ehd->td', g, we2)
        shared = jax.nn.silu(xt @ ws1) * (xt @ ws3) @ ws2
        k = TOP_K
        out = shared / (k + 1) + moe_out * (k / (k + 1))
        return out.reshape(B, S, D)
    x = L0_attn_x
    xn = _layernorm(x, axis=-1)
    x = x + _L0_attn_ref(xn, L0_attn_l_q1, L0_attn_l_k1, L0_attn_l_q2, L0_attn_l_k2, L0_attn_wq, L0_attn_wk, L0_attn_wv, L0_attn_wo) + _L0_ffn_ref(xn, L0_ffn_w_router, L0_ffn_we1, L0_ffn_we3, L0_ffn_we2, L0_ffn_ws1, L0_ffn_ws3, L0_ffn_ws2)
    return x

_drawn_inputs = setup_inputs


def setup_inputs(seed=0):
    import zlib

    import numpy as np

    out = dict(_drawn_inputs(seed))
    spreads = {}
    factors = {'L0_attn_l_k2': 8.0}
    for name, (base, spread) in spreads.items():
        noise = np.random.default_rng([zlib.crc32(name.encode()), seed]).standard_normal(out[name].shape)
        drawn = base * np.exp(spread * noise) if base else spread * noise
        out[name] = jnp.asarray(drawn.astype(out[name].dtype))
    for name, factor in factors.items():
        out[name] = (out[name] * factor).astype(out[name].dtype)
    return out
```

```python
from contextlib import ExitStack
import math

import concourse.bass as bass
from concourse import mybir

F32 = mybir.dt.float32
F32R = mybir.dt.float32r
BF16 = mybir.dt.bfloat16
ALU = mybir.AluOpType
ACT = mybir.ActivationFunctionType
AX_X = mybir.AxisListType.X

P = 128
B, S, D = 4, 1024, 256
T = B * S
DC = D // P
NH = 8
DH = D // NH
NPAIR = B * NH
QB = S // P
GRP = 512
NG = T // GRP
GT = GRP // P
E, TOP_K, H, HS = 16, 4, 128, 512
NX = E + HS // H
NORM_G = DH // NH
L_INIT = 0.8 - 0.6 * math.exp(-0.3 * 1)
RMS_EPS = 1e-6
LN_EPS = 1e-5
SCALE = 1.0 / math.sqrt(DH)
MASKED = -1e30
NP = 4
STK = 3 * DH
NSTEP = 2 * QB
PARTS = [(h, i, k, min(k + GRP, (i + 1) * P)) for h in range(2) for i in range(QB)
         for k in range(0, (i + 1) * P, GRP)]
NPART = len(PARTS)
SIDE = {2: range(0, 4), 3: range(4, 8), 4: range(8, 12), 5: range(12, 16), 6: range(16, 20), 7: range(20, NPART)}


def wait(eng, sem, count):
    if not isinstance(count, int) or count > 0:
        eng.wait_ge(sem, count)


def build(nc, x, lq1, lk1, lq2, lk2, wqT, wkT, wvT, woT, wr, we1, we3, we2, ws1, ws3, ws2, out, o_dram):
    with ExitStack() as whole:
        keep = lambda n, s, d=F32: whole.enter_context(nc.sbuf_tensor(n, s, d))
        sem = lambda n: whole.enter_context(nc.semaphore(n))

        xT_hi = keep("xT_hi", [P, DC, T], F32R)
        xT_lo = keep("xT_lo", [P, DC, T], F32R)
        cw_hl = keep("cw_hl", [P, T // P, 2 * E])
        gate = keep("gate", [P, T // P, E])
        ident = keep("ident", [P, P])
        ident_b = keep("ident_b", [P, P], BF16)
        neg_lam = keep("neg_lam", [P, 1])
        rms_eps = keep("rms_eps", [P, 1])
        x_tiles = x.rearrange("b (g t p) d -> (b g) p t d", p=P, t=GT)
        out_tiles = out.rearrange("b (g t p) d -> (b g) p t d", p=P, t=GT)

        with ExitStack() as early:
            v_all = early.enter_context(nc.sbuf_tensor("v_all", [P, T // P, D], F32))
            scores_r = early.enter_context(nc.sbuf_tensor("scores_r", [P, T // P, E], F32))
            with ExitStack() as ctx:
                project_tokens(nc, ctx, x_tiles, (lq1, lk1, lq2, lk2), wvT, wr, xT_hi, xT_lo, v_all, scores_r, gate, ident,
                               ident_b, neg_lam, rms_eps)
            with ExitStack() as ctx:
                attention(nc, ctx, wqT, wkT, xT_hi, xT_lo, v_all, scores_r, gate, cw_hl, ident, ident_b, neg_lam, o_dram)
        with ExitStack() as ctx:
            feed_forward(nc, ctx, x_tiles, out_tiles, o_dram, woT, we1, we3, we2, ws1, ws3, ws2, xT_hi, xT_lo,
                         gate, cw_hl, ident, rms_eps)


def project_tokens(nc, ctx, x_tiles, lams, wvT, wr, xT_hi, xT_lo, v_all, scores_r, gate, ident, ident_b, neg_lam, rms_eps):
    sb = lambda n, s, d=F32: ctx.enter_context(nc.sbuf_tensor(n, s, d))
    sem = lambda n: ctx.enter_context(nc.semaphore(n))
    NV = D + E
    x_in = sb("x_in", [P, 2, GT, D])
    xn = sb("xn", [P, 2, GT, D])
    stats = sb("stats", [P, 2, GT, 6])
    mean_var = sb("mean_var", [P, 2, GT, 2])
    std = sb("std", [P, 2, GT])
    rstd = sb("rstd", [P, 2, GT])
    st_hi = sb("st_hi", [P, 2, DC, GRP], F32R)
    st_lo = sb("st_lo", [P, 2, DC, GRP], F32R)
    wv_raw = sb("wv_raw", [P, DC, NV])
    wv_hi = sb("wv_hi", [P, DC, NV], F32R)
    wv_lo = sb("wv_lo", [P, DC, NV], F32R)
    lam_in = sb("lam_in", [P, 4, NH])
    lam_prod = sb("lam_prod", [P, 2, NH])
    lam_sum = sb("lam_sum", [P, 2])
    lam_exp = sb("lam_exp", [P, 2])
    ln_eps = sb("ln_eps", [P, 1])
    top = sb("top", [P, T // P])
    shifted = sb("shifted", [P, T // P, E])
    ps_t = [ctx.enter_context(nc.psum_tensor(f"ps_t{i}", [P, DC, GRP], F32)) for i in range(2)]
    ps_v = ctx.enter_context(nc.psum_tensor("ps_v", [P, GT, 512], F32))

    x_loaded = [sem(f"x_loaded{i}") for i in range(2)]
    wv_loaded, lam_loaded = sem("wv_loaded"), sem("lam_loaded")
    zeroed, consts, ident_made = sem("zeroed"), sem("consts"), sem("ident_made")
    wv_rounded, wv_split = sem("wv_rounded"), sem("wv_split")
    bn_done, stats_done, std_done, rstd_done, xn_done = (sem(n) for n in (
        "bn_done", "stats_done", "std_done", "rstd_done", "xn_done"))
    xt_in_psum, hi_done, lo_done, v_in_psum, v_copied, r_copied = (sem(n) for n in (
        "xt_in_psum", "hi_done", "lo_done", "v_in_psum", "v_copied", "r_copied"))
    kept = [sem(f"kept{i}") for i in range(2)]
    lam_a, lam_b, lam_c, lam_d = (sem(n) for n in ("lam_a", "lam_b", "lam_c", "lam_d"))
    top_done, shift_done, gate_done = (sem(n) for n in ("top_done", "shift_done", "gate_done"))

    block = ctx.enter_context(nc.Block())

    @block.sync
    def _(sp):
        sp.dma_start(wv_raw[:, :, 0:D], wvT.rearrange("(c p) n -> p c n", p=P)).then_inc(wv_loaded, 16)
        sp.dma_start(wv_raw[:, :, D:NV], wr.rearrange("(c p) n -> p c n", p=P)).then_inc(wv_loaded, 16)
        for i, lam in enumerate(lams):
            sp.dma_start(lam_in[:, i, :], lam.partition_broadcast(P)).then_inc(lam_loaded, 16)
        for g in range(2):
            sp.dma_start(x_in[:, g], x_tiles[g]).then_inc(x_loaded[g], 16)
        with sp.Fori(0, NG // 2) as trip:
            g0 = trip * 2
            for p in range(2):
                sp.wait_ge(lo_done, g0 + p + 1)
                cols = bass.ds((g0 + p) * GRP, GRP)
                sp.dma_start(xT_hi[:, :, cols].bitcast(F32), st_hi[:, p].bitcast(F32)).then_inc(kept[p], 16)
                sp.dma_start(xT_lo[:, :, cols].bitcast(F32), st_lo[:, p].bitcast(F32)).then_inc(kept[p], 16)
                sp.wait_ge(xn_done, g0 + p + 1)
                sp.dma_start(x_in[:, p], x_tiles[bass.ds((g0 + p + 2) % NG, 1)].rearrange("g p t d -> (g p) t d")
                             ).then_inc(x_loaded[p], 16)
        for p in range(2):
            sp.wait_ge(kept[p], 16 * NG)
            sp.wait_ge(x_loaded[p], 16 * (NG // 2 + 1))

    @block.gpsimd
    def _(pool):
        pool.memset(ident[:], 0.0).then_inc(zeroed, 1)
        pool.wait_ge(zeroed, 1)
        pool.affine_select(out=ident[:], in_=ident[:], compare_op=ALU.not_equal, fill=1.0, base=0,
                           pattern=[[-1, P]], channel_multiplier=1).then_inc(ident_made, 1)
        pool.wait_ge(ident_made, 1)
        pool.tensor_copy(ident_b[:], ident[:]).then_inc(ident_made, 1)

    @block.vector
    def _(dve):
        nc.vector.memset(ln_eps[:], LN_EPS).then_inc(consts, 1)
        nc.vector.memset(rms_eps[:], RMS_EPS).then_inc(consts, 1)
        dve.wait_ge(wv_rounded, 1)
        nc.vector.tensor_tensor(wv_lo[:], wv_raw[:], wv_hi[:].bitcast(F32), ALU.subtract).then_inc(wv_split, 1)
        dve.wait_ge(lam_loaded, 64)
        nc.vector.tensor_tensor(lam_prod[:], lam_in[:, 0::2, :], lam_in[:, 1::2, :], ALU.mult).then_inc(lam_a, 1)
        dve.wait_ge(lam_a, 1)
        nc.vector.tensor_reduce(lam_sum[:], lam_prod[:], AX_X, ALU.add).then_inc(lam_b, 1)
        dve.wait_ge(lam_c, 1)
        nc.vector.tensor_tensor(neg_lam[:], lam_exp[:, 1:2], lam_exp[:, 0:1], ALU.subtract).then_inc(lam_d, 1)
        dve.wait_ge(lam_d, 1)
        nc.vector.tensor_scalar(neg_lam[:], neg_lam[:], -L_INIT, None, ALU.add).then_inc(lam_d, 1)

        def token_stats(g0, p):
            dve.wait_ge(x_loaded[p], g0 * 8 + 16)
            if p:
                dve.wait_ge(bn_done, g0 + p)
            for t in range(GT):
                last = nc.vector.bn_stats(stats[:, p, t, :], x_in[:, p, t, :])
            last.then_inc(bn_done, 1)

        def combine_stats(p):
            for t in range(GT):
                last = nc.vector.bn_aggr(mean_var[:, p, t, :], stats[:, p, t, :])
            last.then_inc(stats_done, 1)

        def invert_std(g0, p):
            if p == 0:
                dve.wait_ge(bn_done, g0 + 2)
            dve.wait_ge(std_done, g0 + p + 1)
            nc.vector.reciprocal(rstd[:, p], std[:, p]).then_inc(rstd_done, 1)

        def normalise(g0, p):
            dve.wait_ge(rstd_done, g0 + p + 1)
            dve.wait_ge(xt_in_psum, g0)
            for t in range(GT):
                last = nc.vector.tensor_scalar(xn[:, p, t, :], x_in[:, p, t, :], mean_var[:, p, t, 0:1],
                                               rstd[:, p, t:t + 1], ALU.subtract, ALU.mult)
            last.then_inc(xn_done, 1)

        def low_part(g, p):
            dve.wait_ge(hi_done, g + 1)
            nc.vector.tensor_tensor(st_lo[:, p], ps_t[p][:], st_hi[:, p].bitcast(F32), ALU.subtract
                                    ).then_inc(lo_done, 1)

        def router_out(g):
            dve.wait_ge(v_in_psum, g + 1)
            dve.wait_ge(v_copied, g + 1)
            nc.vector.tensor_copy(scores_r[:, bass.ds(g * GT, GT), :], ps_v[:, :, D:NV]).then_inc(r_copied, 1)

        with dve.Fori(0, NG // 2) as trip:
            g0 = trip * 2
            token_stats(g0, 0)
            token_stats(g0, 1)
            combine_stats(0)
            invert_std(g0, 0)
            combine_stats(1)
            normalise(g0, 0)
            invert_std(g0, 1)
            normalise(g0, 1)
            for p in range(2):
                low_part(g0 + p, p)
            for p in range(2):
                router_out(g0 + p)
        dve.wait_ge(r_copied, NG)
        nc.vector.tensor_reduce(top[:], scores_r[:], AX_X, ALU.max).then_inc(top_done, 1)
        dve.wait_ge(top_done, 1)
        nc.vector.tensor_tensor(shifted[:], scores_r[:], top[:].unsqueeze(2).broadcast_to([P, T // P, E]),
                                ALU.subtract).then_inc(shift_done, 1)

    @block.scalar
    def _(act):
        act.wait_ge(wv_loaded, 32)
        nc.scalar.activation(wv_hi[:], wv_raw[:], ACT.Copy).then_inc(wv_rounded, 1)
        act.wait_ge(lam_b, 1)
        nc.scalar.activation(lam_exp[:], lam_sum[:], ACT.Exp).then_inc(lam_c, 1)
        act.wait_ge(consts, 2)
        with act.Fori(0, NG // 2) as trip:
            g0 = trip * 2
            for p in range(2):
                act.wait_ge(stats_done, g0 + p + 1)
                nc.scalar.activation(std[:, p], mean_var[:, p, :, 1], ACT.Sqrt, bias=ln_eps[:]).then_inc(std_done, 1)
            for p in range(2):
                act.wait_ge(xt_in_psum, g0 + p + 1)
                act.wait_ge(kept[p], g0 * 16)
                nc.scalar.activation(st_hi[:, p], ps_t[p][:], ACT.Copy).then_inc(hi_done, 1)
            for p in range(2):
                act.wait_ge(v_in_psum, g0 + p + 1)
                nc.scalar.activation(v_all[:, bass.ds((g0 + p) * GT, GT), :], ps_v[:, :, 0:D], ACT.Copy
                                     ).then_inc(v_copied, 1)
        act.wait_ge(shift_done, 1)
        nc.scalar.activation(gate[:], shifted[:], ACT.Exp).then_inc(gate_done, 1)

    @block.tensor
    def _(pe):
        pe.wait_ge(ident_made, 1)

        def transposes(g, p):
            pe.wait_ge(xn_done, g + 1)
            pe.wait_ge(lo_done, g - p)
            for c in range(DC):
                for t in range(GT):
                    last = nc.tensor.transpose(ps_t[p][:, c, t * P:(t + 1) * P], xn[:, p, t, c * P:(c + 1) * P],
                                               ident[:])
            last.then_inc(xt_in_psum, 1)

        def values(g, p):
            pe.wait_ge(lo_done, g + 1)
            pe.wait_ge(v_copied, g)
            pe.wait_ge(r_copied, g)
            for t in range(GT):
                cols = slice(t * P, (t + 1) * P)
                n = 0
                for c in range(DC):
                    for a, b in ((st_hi, wv_hi), (st_hi, wv_lo), (st_lo, wv_hi)):
                        n += 1
                        last = nc.tensor.matmul(ps_v[:, t, 0:NV], a[:, p, c, cols], b[:, c, :],
                                                start=(n == 1), stop=(n == 3 * DC))
            last.then_inc(v_in_psum, 1)

        first = True
        with pe.Fori(0, NG // 2) as trip:
            g0 = trip * 2
            for p in range(2):
                transposes(g0 + p, p)
            if first:
                pe.wait_ge(wv_split, 1)
                first = False
            for p in range(2):
                values(g0 + p, p)


def attention(nc, ctx, wqT, wkT, xT_hi, xT_lo, v_all, scores_r, gate, cw_hl, ident, ident_b, neg_lam, o_dram):
    sb = lambda n, s, d=F32: ctx.enter_context(nc.sbuf_tensor(n, s, d))
    sem = lambda n: ctx.enter_context(nc.semaphore(n))
    w_raw = sb("w_raw", [P, DC, P])
    w_hi = sb("w_hi", [P, DC, P], F32R)
    w_lo = sb("w_lo", [P, DC, P], F32R)
    qk_hi = sb("qk_hi", [P, S], F32R)
    qk_lo = sb("qk_lo", [P, S], F32R)
    stack = sb("stack", [P, 2, 4, S], F32R)
    v_ones = sb("v_ones", [P, 2, QB, 2 * DH])
    probs = sb("probs", [P, NP, S])
    part_max = sb("part_max", [P, 2, 2 * QB, 2])
    row_max = sb("row_max", [P, 2, 2 * QB])
    max_row = sb("max_row", [2 * QB, P], F32R)
    o_raw = sb("o_raw", [P, S])
    rden = sb("rden", [P, QB, 2])
    rlam = sb("rlam", [P, QB])
    o_a = sb("o_a", [P, QB, DH])
    o_b = sb("o_b", [P, QB, DH])
    o_pair = sb("o_pair", [P, 2, QB, DH])
    mask_f = sb("mask_f", [P, 2, P])
    mask_qk = sb("mask_qk", [P, P], BF16)
    mask_kq = sb("mask_kq", [P, P], BF16)
    rank = sb("rank", [P, T // P, E])
    beats = sb("beats", [P, T // P, E])
    ps_s = [ctx.enter_context(nc.psum_tensor(f"ps_s{i}", [P, S], F32)) for i in range(2)]
    ps_x = ctx.enter_context(nc.psum_tensor("ps_x", [P, S], F32))
    ps_o = ctx.enter_context(nc.psum_tensor("ps_o", [P, S], F32))

    w_loaded, w_rounded, w_split = sem("w_loaded"), sem("w_rounded"), sem("w_split")
    mask_0, mask_1, mask_2, ones_a, ones_b = (sem(n) for n in ("mask_0", "mask_1", "mask_2", "ones_a", "ones_b"))
    projected, hi_out, lo_out, stacked = (sem(n) for n in ("projected", "hi_out", "lo_out", "stacked"))
    side_scores, side_max, max_joined, max_filled, max_in_psum, max_turned, max_placed = (sem(n) for n in (
        "side_scores", "side_max", "max_joined", "max_filled", "max_in_psum", "max_turned", "max_placed"))
    scored, exped, pv_done, v_staged = (sem(n) for n in ("scored", "exped", "pv_done", "v_staged"))
    o_copied, o_turned, rden_done, rlam_done, oa_done, ob_done, o_done = (sem(n) for n in (
        "o_copied", "o_turned", "rden_done", "rlam_done", "oa_done", "ob_done", "o_done"))
    o_stored = [sem(f"o_stored{i}") for i in range(2)]
    ranked, v_filled = sem("ranked"), sem("v_filled")

    Q, K = (0, 2), (1, 3)
    o_view = o_dram.rearrange("(b i p) d -> b p i d", p=P, i=QB)

    block = ctx.enter_context(nc.Block())
    TRIPS = (NPAIR - 4) // 2

    @block.sync
    def _(sp):
        def load_weights(n):
            wait(sp, w_split, n)
            for h in range(2):
                for i, w in enumerate((wqT, wkT)):
                    src = w.rearrange("(c p) (h j f) -> p c h j f", p=P, h=2, f=DH)
                    src = src[:, :, h, bass.ds(n % NH, 1), :].rearrange("p c j f -> p c (j f)")
                    at = (2 * i + h) * DH
                    sp.dma_start(w_raw[:, :, at:at + DH], src).then_inc(w_loaded, 16)

        def stack_pair(n, p, first=False):
            sp.wait_ge(lo_out, n + 1)
            if not first:
                wait(sp, scored, NSTEP * (n - 1))
            for h in range(2):
                q, k = h * DH, (2 + h) * DH
                for src, row, place, at in ((qk_hi, q, Q[h], 0), (qk_lo, q, Q[h], DH), (qk_hi, q, Q[h], 2 * DH),
                                            (qk_hi, k, K[h], 0), (qk_hi, k, K[h], DH), (qk_lo, k, K[h], 2 * DH)):
                    sp.dma_start(stack[at:at + DH, p, place, :].bitcast(F32),
                                 src[row:row + DH, :].bitcast(F32)).then_inc(stacked, 16)

        def place_max(n, p):
            sp.wait_ge(max_turned, n + 1)
            for h in range(2):
                sp.dma_start(stack[STK:STK + 1, p, Q[h], :].bitcast(F32),
                             max_row[h * QB:(h + 1) * QB, :].bitcast(F32)).then_inc(max_placed, 16)

        def store(n, p):
            sp.wait_ge(o_done, n + 1)
            dst = o_view[bass.ds(n // NH, 1), :, :, bass.ds((n % NH) * DH, DH)].rearrange("b p i d -> (b p) i d")
            sp.dma_start(dst, o_pair[:, p]).then_inc(o_stored[p], 16)

        def step(n, p, stack_next=True, store_last=True, weights=True):
            if stack_next:
                stack_pair(n + 1, 1 - p)
            if weights:
                load_weights(n + 3)
            if store_last:
                store(n - 1, 1 - p)
            if stack_next:
                place_max(n + 1, 1 - p)

        load_weights(0)
        stack_pair(0, 0, first=True)
        load_weights(1)
        place_max(0, 0)
        load_weights(2)
        stack_pair(1, 1, first=True)
        load_weights(3)
        place_max(1, 1)
        with sp.Fori(0, TRIPS) as trip:
            n = trip * 2 + 1
            step(n, 1)
            step(n + 1, 0)
        step(NPAIR - 3, 1, weights=False)
        step(NPAIR - 2, 0, weights=False)
        step(NPAIR - 1, 1, stack_next=False, weights=False)
        store(NPAIR - 1, 1)
        for p in range(2):
            sp.wait_ge(o_stored[p], 16 * (NPAIR // 2))

    @block.gpsimd
    def _(pool):
        pool.memset(mask_f[:], 0.0).then_inc(mask_0, 1)
        pool.wait_ge(mask_0, 1)
        pool.affine_select(out=mask_f[:, 0, :], in_=mask_f[:, 0, :], compare_op=ALU.is_ge, fill=MASKED, base=0,
                           pattern=[[-1, P]], channel_multiplier=1).then_inc(mask_1, 1)
        pool.affine_select(out=mask_f[:, 1, :], in_=mask_f[:, 1, :], compare_op=ALU.is_ge, fill=MASKED, base=0,
                           pattern=[[1, P]], channel_multiplier=-1).then_inc(mask_1, 1)
        pool.wait_ge(mask_1, 2)
        pool.tensor_copy(mask_qk[:], mask_f[:, 0, :]).then_inc(mask_2, 1)
        pool.tensor_copy(mask_kq[:], mask_f[:, 1, :]).then_inc(mask_2, 1)
        pool.memset(v_ones[:], 1.0).then_inc(v_filled, 1)
        pool.wait_ge(v_filled, 1)

        def stage_values(n, p, wait=True):
            if wait:
                pool.wait_ge(pv_done, QB * (n - 1))
            pool.tensor_copy(v_ones[:, p, :, 0:DH],
                             v_all[:, bass.ds((n // NH) * QB, QB), bass.ds((n % NH) * DH, DH)]).then_inc(v_staged, 1)

        stage_values(0, 0, wait=False)
        stage_values(1, 1, wait=False)
        with pool.Fori(1, NPAIR // 2) as trip:
            n = trip * 2
            stage_values(n, 0)
            stage_values(n + 1, 1)

    @block.tensor
    def _(pe):
        def project(n):
            pe.wait_ge(w_split, n + 1)
            wait(pe, side_max, NPART * n)
            col = (n // NH) * S
            for half in range(2):
                k = 0
                for c in range(DC):
                    for w, xt in ((w_hi, xT_hi), (w_lo, xT_hi), (w_hi, xT_lo)):
                        k += 1
                        last = nc.tensor.matmul(ps_x[:, half * GRP:(half + 1) * GRP], w[:, c, :],
                                                xt[:, c, bass.ds(col + half * GRP, GRP)],
                                                start=(k == 1), stop=(k == 3 * DC))
            last.then_inc(projected, 1)

        def side(n, p, m):
            h, i, k0, k1 = PARTS[m]
            if m == 0:
                pe.wait_ge(stacked, 192 * (n + 1))
            if m >= 2:
                pe.wait_ge(side_max, NPART * n + m - 1)
            at = (m % 2) * GRP
            diag = k1 == (i + 1) * P
            last = nc.tensor.matmul(ps_x[:, at:at + k1 - k0], stack[0:STK, p, Q[h], i * P:(i + 1) * P],
                                    stack[0:STK, p, K[h], k0:k1], start=True, stop=not diag)
            if diag:
                last = nc.tensor.matmul(ps_x[:, at + k1 - k0 - P:at + k1 - k0], ident_b[:], mask_qk[:],
                                        start=False, stop=True)
            last.then_inc(side_scores, 1)

        def turn_max(n, p):
            pe.wait_ge(max_joined, n + 1)
            if not (isinstance(n, int) and n == 0):
                pe.wait_ge(exped, NSTEP * n)
            nc.tensor.transpose(ps_s[0][0:2 * QB, 0:P], row_max[:, p, :], ident[:]).then_inc(max_in_psum, 1)

        def score(n, p, c, h):
            s = 2 * c + h
            if s == 0:
                pe.wait_ge(max_placed, 32 * (n + 1))
            if not (isinstance(n, int) and n == 0 and s < 2):
                pe.wait_ge(exped, NSTEP * n + s - 1)
            ps = ps_s[h]
            q0 = c * P
            while q0 < S:
                q1 = min((q0 // GRP + 1) * GRP, S)
                diag = q0 == c * P
                last = nc.tensor.matmul(ps[:, q0:q1], stack[0:STK + 1, p, K[h], c * P:(c + 1) * P],
                                        stack[0:STK + 1, p, Q[h], q0:q1], start=True, stop=not diag)
                if diag:
                    last = nc.tensor.matmul(ps[:, q0:q0 + P], ident_b[:], mask_kq[:], start=False, stop=True)
                q0 = q1
            last.then_inc(scored, 1)

        def value(n, p, c):
            if c == 0:
                pe.wait_ge(v_staged, n + 1)
                wait(pe, o_copied, n)
            pe.wait_ge(exped, NSTEP * n + 2 * c + 2)
            q0 = c * P
            while q0 < S:
                q1 = min((q0 // GRP + 1) * GRP, S)
                for h in range(2):
                    last = nc.tensor.matmul(ps_o[h * 64:(h + 1) * 64, q0:q1], v_ones[:, p, c, :],
                                            probs[:, (2 * c + h) % NP, q0:q1], start=(c == 0),
                                            stop=(c * P + P >= q1))
                q0 = q1
            last.then_inc(pv_done, 1)

        def turn_out(n):
            pe.wait_ge(o_copied, n + 1)
            pe.wait_ge(lo_out, n + 3 if not isinstance(n, int) else min(n + 3, NPAIR))
            for i in range(QB):
                last = nc.tensor.transpose(ps_x[:, i * P:(i + 1) * P], o_raw[:, i * P:(i + 1) * P], ident[:])
            last.then_inc(o_turned, 1)

        def step(n, p, sides=True, projects=True, turns=True):
            for c in range(QB):
                todo = list(SIDE.get(c, ())) if sides else []
                if todo and todo[0] == 0:
                    pe.wait_ge(o_done, n) if turns else pe.wait_ge(lo_out, 2)
                for h in range(2):
                    score(n, p, c, h)
                    if todo:
                        side(n + 1, 1 - p, todo.pop(0))
                if c == 0 and turns:
                    turn_out(n - 1)
                if c > 0:
                    value(n, p, c - 1)
                for m in todo:
                    side(n + 1, 1 - p, m)
            value(n, p, QB - 1)
            if sides:
                turn_max(n + 1, 1 - p)
            if projects:
                project(n + 2)

        pe.wait_ge(ones_b, 1)
        pe.wait_ge(mask_2, 2)
        project(0)
        pe.wait_ge(lo_out, 1)
        for m in range(NPART):
            side(0, 0, m)
        turn_max(0, 0)
        project(1)
        step(0, 0, turns=False)
        with pe.Fori(0, TRIPS) as trip:
            n = trip * 2 + 1
            step(n, 1)
            step(n + 1, 0)
        step(NPAIR - 3, 1)
        step(NPAIR - 2, 0, projects=False)
        step(NPAIR - 1, 1, sides=False, projects=False)
        turn_out(NPAIR - 1)

    @block.scalar
    def _(act):
        def round_weights(n):
            act.wait_ge(w_loaded, 64 * (n + 1))
            wait(act, projected, n)
            nc.scalar.activation(w_hi[:], w_raw[:], ACT.Copy).then_inc(w_rounded, 1)

        def high_part(n):
            act.wait_ge(projected, n + 1)
            wait(act, stacked, 192 * n)
            nc.scalar.activation(qk_hi[:], ps_x[:], ACT.Copy).then_inc(hi_out, 1)

        def exp(n, c, h):
            s = 2 * c + h
            act.wait_ge(scored, NSTEP * n + s + 1)
            if not (isinstance(n, int) and n == 0 and s < NP):
                act.wait_ge(pv_done, QB * n + c - NP // 2 + 1)
            nc.scalar.activation(probs[:, s % NP, c * P:S], ps_s[h][:, c * P:S], ACT.Exp, scale=SCALE
                                 ).then_inc(exped, 1)

        def step(n, projects=True):
            for c in range(QB):
                for h in range(2):
                    exp(n, c, h)
            if projects:
                high_part(n + 2)
                round_weights(n + 3) if not isinstance(n, int) or n + 3 < NPAIR else None

        round_weights(0)
        act.wait_ge(ones_a, 1)
        for p in range(2):
            for h in range(2):
                last = nc.scalar.activation(stack[STK:STK + 1, p, K[h], :], o_raw[STK:STK + 1, :], ACT.Copy)
        last.then_inc(ones_b, 1)
        high_part(0)
        round_weights(1)
        high_part(1)
        round_weights(2)
        step(0)
        with act.Fori(0, TRIPS) as trip:
            n = trip * 2 + 1
            step(n)
            step(n + 1)
        step(NPAIR - 3)
        step(NPAIR - 2, projects=False)
        step(NPAIR - 1, projects=False)

    @block.vector
    def _(dve):
        def split_weights(n):
            dve.wait_ge(w_rounded, n + 1)
            nc.vector.tensor_tensor(w_lo[:], w_raw[:], w_hi[:].bitcast(F32), ALU.subtract).then_inc(w_split, 1)

        def low_part(n):
            dve.wait_ge(hi_out, n + 1)
            nc.vector.tensor_tensor(qk_lo[:], ps_x[:], qk_hi[:].bitcast(F32), ALU.subtract).then_inc(lo_out, 1)

        def side_maxima(n, p, m):
            h, i, k0, k1 = PARTS[m]
            at = (m % 2) * GRP
            dve.wait_ge(side_scores, NPART * n + m + 1)
            nc.vector.tensor_reduce(part_max[:, p, h * QB + i, k0 // GRP:k0 // GRP + 1], ps_x[:, at:at + k1 - k0],
                                    AX_X, ALU.max).then_inc(side_max, 1)

        def join_maxima(n, p):
            dve.wait_ge(side_max, NPART * (n + 1))
            nc.vector.tensor_reduce(row_max[:, p, :], part_max[:, p], AX_X, ALU.max).then_inc(max_joined, 1)

        def negate_max(n):
            dve.wait_ge(max_in_psum, n + 1)
            wait(dve, max_placed, 32 * n)
            nc.vector.tensor_scalar(max_row[:], ps_s[0][0:2 * QB, 0:P], -1.0, None, ALU.mult).then_inc(max_turned, 1)

        def copy_out(n):
            dve.wait_ge(pv_done, QB * (n + 1))
            nc.vector.tensor_copy(o_raw[:], ps_o[:]).then_inc(o_copied, 1)

        def combine(n, p):
            turned = ps_x[:].rearrange("q (i f) -> q i f", f=P)
            dve.wait_ge(o_turned, n + 1)
            nc.vector.reciprocal(rden[:], turned[:, :, DH::2 * DH]).then_inc(rden_done, 1)
            dve.wait_ge(rden_done, n + 1)
            nc.vector.tensor_scalar(rlam[:], rden[:, :, 1], neg_lam[:, 0:1], None, ALU.mult).then_inc(rlam_done, 1)
            nc.vector.tensor_tensor(o_a[:], turned[:, :, 0:DH], rden[:, :, 0:1].broadcast_to([P, QB, DH]), ALU.mult
                                    ).then_inc(oa_done, 1)
            dve.wait_ge(rlam_done, n + 1)
            nc.vector.tensor_tensor(o_b[:], turned[:, :, 2 * DH:3 * DH],
                                    rlam[:].unsqueeze(2).broadcast_to([P, QB, DH]), ALU.mult).then_inc(ob_done, 1)
            dve.wait_ge(oa_done, n + 1)
            dve.wait_ge(ob_done, n + 1)
            if not (isinstance(n, int) and n < 2):
                dve.wait_ge(o_stored[p], (n // 2) * 16)
            nc.vector.tensor_tensor(o_pair[:, p], o_a[:], o_b[:], ALU.add).then_inc(o_done, 1)

        def step(n, p, sides=True, projects=True, turns=True):
            if turns:
                combine(n - 1, 1 - p)
            if sides:
                for m in range(NPART):
                    side_maxima(n + 1, 1 - p, m)
                join_maxima(n + 1, 1 - p)
            copy_out(n)
            if sides:
                negate_max(n + 1)
            if projects:
                low_part(n + 2)
                if not isinstance(n, int) or n + 3 < NPAIR:
                    split_weights(n + 3)

        nc.vector.memset(o_raw[STK:STK + 1, :], 1.0).then_inc(ones_a, 1)
        nc.vector.memset(part_max[:], -3e38).then_inc(max_filled, 1)
        dve.wait_ge(max_filled, 1)
        split_weights(0)
        low_part(0)
        split_weights(1)
        for m in range(NPART):
            side_maxima(0, 0, m)
        join_maxima(0, 0)
        negate_max(0)
        low_part(1)
        split_weights(2)
        step(0, 0, turns=False)
        with dve.Fori(0, TRIPS) as trip:
            n = trip * 2 + 1
            step(n, 1)
            step(n + 1, 0)
        step(NPAIR - 3, 1)
        step(NPAIR - 2, 0, projects=False)
        nc.vector.memset(rank[:], 0.0).then_inc(ranked, 1)
        count = 1
        for f in range(E):
            dve.wait_ge(ranked, count)
            for lo, hi, op in ((0, f + 1, ALU.is_gt), (f + 1, E, ALU.is_ge)):
                if hi > lo:
                    last = nc.vector.tensor_tensor(
                        beats[:, :, lo:hi], scores_r[:, :, f:f + 1].broadcast_to([P, T // P, hi - lo]),
                        scores_r[:, :, lo:hi], op)
            last.then_inc(ranked, 1)
            dve.wait_ge(ranked, count + 1)
            nc.vector.tensor_tensor(rank[:], rank[:], beats[:], ALU.add).then_inc(ranked, 1)
            count += 2
        dve.wait_ge(ranked, count)
        nc.vector.scalar_tensor_tensor(out=gate[:], in0=rank[:], scalar=TOP_K - 0.5, in1=gate[:], op0=ALU.is_lt,
                                       op1=ALU.mult).then_inc(ranked, 1)
        step(NPAIR - 1, 1, sides=False, projects=False)
        combine(NPAIR - 1, 1)


def feed_forward(nc, ctx, x_tiles, out_tiles, o_dram, woT, we1, we3, we2, ws1, ws3, ws2, xT_hi, xT_lo, gate, cw_hl,
                 ident, rms_eps):
    sb = lambda n, s, d=F32: ctx.enter_context(nc.sbuf_tensor(n, s, d))
    sem = lambda n: ctx.enter_context(nc.semaphore(n))
    work = sb("work", [P, 4, GRP])
    w13_raw = work[:, 0:2, :].rearrange("p b (i c h) -> p b i c h", i=2, c=DC)
    hid, mid = work[:, 0:2, :], work[:, 2:4, :]
    w13_hi = sb("w13_hi", [P, NX, 2, DC, H], F32R)
    w13_lo = sb("w13_lo", [P, NX, 2, DC, H], F32R)
    w2 = sb("w2", [P, NX, D])
    wo = sb("wo", [P, DC, D])
    pick_f = sb("pick_f", [2 * E, E])
    pick = sb("pick", [2 * E, E], F32R)
    gate_sum = sb("gate_sum", [P, T // P])
    gate_inv = sb("gate_inv", [P, T // P])
    cw_st = sb("cw_st", [P, GT, 2 * E])
    cwT = sb("cwT", [2 * E, GRP], F32R)
    o_in = sb("o_in", [P, GT, D])
    ms = sb("ms", [P, GT, D // NORM_G])
    on = sb("on", [P, GT, D])
    oT = sb("oT", [P, DC, GRP])
    res = sb("res", [P, GT, D])
    act_h = sb("act_h", [P, 2, GRP])
    ps_h = [ctx.enter_context(nc.psum_tensor(f"ps_h{i}", [P, 2, GRP], F32)) for i in range(2)]
    ps_c = ctx.enter_context(nc.psum_tensor("ps_c", [P, 2, GRP], F32))
    ps_y = ctx.enter_context(nc.psum_tensor("ps_y", [P, GT, D], F32))

    raw_loaded = [sem(f"raw_loaded{i}") for i in range(2)]
    w2_loaded, raw_hi, raw_lo = sem("w2_loaded"), sem("raw_hi"), sem("raw_lo")
    pick_0, pick_1, pick_2 = (sem(n) for n in ("pick_0", "pick_1", "pick_2"))
    gs, gi, gc, gh, gl = (sem(n) for n in ("gs", "gi", "gc", "gh", "gl"))
    cw_staged, cw_turned, cwT_done = (sem(n) for n in ("cw_staged", "cw_turned", "cwT_done"))
    o_loaded, x_loaded, sq_done, ms_done, rms_done, rr_done, on_done, o_turned, oT_done = (sem(n) for n in (
        "f_o_loaded", "f_x_loaded", "sq_done", "ms_done", "rms_done", "rr_done", "on_done", "f_o_turned", "oT_done"))
    h_ready, c_ready, silu_done, mid_done, hid_done, y_part, res_done, stored = (sem(n) for n in (
        "h_ready", "c_ready", "silu_done", "mid_done", "hid_done", "y_part", "res_done", "stored"))
    o_tiles = o_dram.rearrange("(g t p) d -> g p t d", p=P, t=GT)
    one = lambda ap: ap.rearrange("g p t d -> (g p) t d")

    block = ctx.enter_context(nc.Block())

    @block.sync
    def _(sp):
        sp.dma_start(o_in[:], o_tiles[0]).then_inc(o_loaded, 16)
        sp.dma_start(wo[:], woT.rearrange("(c p) n -> p c n", p=P)).then_inc(w2_loaded, 16)
        for e in range(NX):
            if e >= 2:
                sp.wait_ge(raw_lo, e - 1)
            for i, (w, ws) in enumerate(((we1, ws1), (we3, ws3))):
                src = w[e] if e < E else ws[:, (e - E) * H:(e - E + 1) * H]
                sp.dma_start(w13_raw[:, e % 2, i], src.rearrange("(c p) h -> p c h", p=P)
                             ).then_inc(raw_loaded[e % 2], 16)
            if e == 1:
                sp.dma_start(w2[:, 0:E, :], we2.rearrange("e h d -> h e d")).then_inc(w2_loaded, 16)
                sp.dma_start(w2[:, E:NX, :], ws2.rearrange("(e h) d -> h e d", h=H)).then_inc(w2_loaded, 16)
        with sp.Fori(0, NG) as g:
            sp.wait_ge(stored, g * 16)
            sp.dma_start(res[:], one(x_tiles[bass.ds(g, 1)])).then_inc(x_loaded, 16)
            sp.wait_ge(on_done, g + 1)
            sp.dma_start(o_in[:], one(o_tiles[bass.ds((g + 1) % NG, 1)])).then_inc(o_loaded, 16)
            sp.wait_ge(res_done, g + 1)
            sp.dma_start(one(out_tiles[bass.ds(g, 1)]), res[:]).then_inc(stored, 16)
        sp.wait_ge(stored, 16 * NG)
        sp.wait_ge(o_loaded, 16 * (NG + 1))

    @block.gpsimd
    def _(pool):
        pool.memset(pick_f[:], 0.0).then_inc(pick_0, 1)
        pool.wait_ge(pick_0, 1)
        for i in range(2):
            pool.affine_select(out=pick_f[:], in_=pick_f[:], compare_op=ALU.not_equal, fill=1.0, base=-E * i,
                               pattern=[[-1, E]], channel_multiplier=1).then_inc(pick_1, 1)
            pool.wait_ge(pick_1, i + 1)
        pool.wait_ge(gl, 1)
        with pool.Fori(0, NG) as g:
            pool.wait_ge(cw_turned, g)
            pool.tensor_copy(cw_st[:], cw_hl[:, bass.ds(g * GT, GT), :]).then_inc(cw_staged, 1)

    @block.scalar
    def _(act):
        def round_weights(e):
            act.wait_ge(raw_loaded[e % 2], 32 * (e // 2 + 1))
            nc.scalar.activation(w13_hi[:, e], w13_raw[:, e % 2], ACT.Copy).then_inc(raw_hi, 1)

        def root(g):
            act.wait_ge(ms_done, g + 1)
            nc.scalar.activation(ms[:], ms[:], ACT.Sqrt, scale=1.0 / NORM_G, bias=rms_eps[:]).then_inc(rms_done, 1)

        def silu(g, e, first):
            s = g * NX + e
            act.wait_ge(h_ready, s + 1)
            if not (first and e < 2):
                act.wait_ge(hid_done, s - 1)
            nc.scalar.activation(act_h[:, e % 2, :], ps_h[e % 2][:, 0, :], ACT.Silu).then_inc(silu_done, 1)

        def group(g, first=False):
            root(g)
            act.wait_ge(cw_turned, g + 1)
            nc.scalar.activation(cwT[:], ps_c[0:2 * E, 0, :], ACT.Copy).then_inc(cwT_done, 1)
            act.wait_ge(o_turned, g + 1)
            nc.scalar.activation(oT[:], ps_h[0][:], ACT.Copy).then_inc(oT_done, 1)
            for e in range(NX):
                silu(g, e, first)

        act.wait_ge(pick_1, 2)
        nc.scalar.activation(pick[:], pick_f[:], ACT.Copy).then_inc(pick_2, 1)
        for e in range(NX):
            round_weights(e)
        group(0, first=True)
        with act.Fori(1, NG) as g:
            group(g)

    @block.vector
    def _(dve):
        nc.vector.tensor_reduce(gate_sum[:], gate[:], AX_X, ALU.add).then_inc(gs, 1)
        dve.wait_ge(gs, 1)
        nc.vector.reciprocal(gate_inv[:], gate_sum[:]).then_inc(gi, 1)
        dve.wait_ge(gi, 1)
        nc.vector.scalar_tensor_tensor(out=gate[:], in0=gate[:], scalar=TOP_K / (TOP_K + 1.0),
                                       in1=gate_inv[:].unsqueeze(2).broadcast_to([P, T // P, E]),
                                       op0=ALU.mult, op1=ALU.mult).then_inc(gc, 1)
        dve.wait_ge(gc, 1)
        nc.vector.tensor_copy(cw_hl[:, :, 0:E].bitcast(F32R), gate[:]).then_inc(gh, 1)
        dve.wait_ge(gh, 1)
        nc.vector.tensor_tensor(cw_hl[:, :, E:2 * E], gate[:], cw_hl[:, :, 0:E], ALU.subtract).then_inc(gl, 1)
        for e in range(NX):
            dve.wait_ge(raw_hi, e + 1)
            nc.vector.tensor_tensor(w13_lo[:, e], w13_raw[:, e % 2], w13_hi[:, e].bitcast(F32), ALU.subtract
                                    ).then_inc(raw_lo, 1)

        def normalise(g):
            dve.wait_ge(o_loaded, 16 * (g + 1))
            dve.wait_ge(o_turned, g)
            nc.vector.tensor_tensor(on[:], o_in[:], o_in[:], ALU.mult).then_inc(sq_done, 1)
            dve.wait_ge(sq_done, g + 1)
            dve.wait_ge(rr_done, g)
            nc.vector.tensor_reduce(ms[:], on[:].rearrange("p t (n k) -> p t n k", k=NORM_G), AX_X, ALU.add
                                    ).then_inc(ms_done, 1)
            dve.wait_ge(rms_done, g + 1)
            nc.vector.reciprocal(ms[:], ms[:]).then_inc(rr_done, 1)
            dve.wait_ge(rr_done, g + 1)
            nc.vector.scalar_tensor_tensor(
                out=on[:].rearrange("p t (n k) -> p (t n) k", k=NORM_G),
                in0=o_in[:].rearrange("p t (n k) -> p (t n) k", k=NORM_G), scalar=1.0 - L_INIT,
                in1=ms[:].rearrange("p t n -> p (t n)").unsqueeze(2).broadcast_to([P, GT * D // NORM_G, NORM_G]),
                op0=ALU.mult, op1=ALU.mult).then_inc(on_done, 1)

        def gated(g, e, first):
            s = g * NX + e
            dve.wait_ge(silu_done, s + 1)
            if not (first and e < 2):
                dve.wait_ge(y_part, s - 1)
            if e < E:
                nc.vector.tensor_tensor(mid[:, e % 2, :], ps_h[e % 2][:, 1, :], act_h[:, e % 2, :], ALU.mult
                                        ).then_inc(mid_done, 1)
                dve.wait_ge(mid_done, g * E + e + 1)
                dve.wait_ge(c_ready, g * E + e + 1)
                nc.vector.tensor_tensor(hid[:, e % 2, :], ps_c[:, e % 2, :], mid[:, e % 2, :], ALU.mult
                                        ).then_inc(hid_done, 1)
            else:
                nc.vector.scalar_tensor_tensor(out=hid[:, e % 2, :], in0=ps_h[e % 2][:, 1, :],
                                               scalar=1.0 / (TOP_K + 1.0), in1=act_h[:, e % 2, :],
                                               op0=ALU.mult, op1=ALU.mult).then_inc(hid_done, 1)

        def group(g, first=False):
            normalise(g)
            for e in range(NX):
                gated(g, e, first)
            dve.wait_ge(y_part, NX * (g + 1))
            dve.wait_ge(x_loaded, 16 * (g + 1))
            nc.vector.tensor_tensor(res[:], ps_y[:], res[:], ALU.add).then_inc(res_done, 1)

        group(0, first=True)
        with dve.Fori(1, NG) as g:
            group(g)

    @block.tensor
    def _(pe):
        def turn(g):
            pe.wait_ge(cw_staged, g + 1)
            pe.wait_ge(hid_done, g * NX)
            for t in range(GT):
                last = nc.tensor.transpose(ps_c[0:2 * E, 0, t * P:(t + 1) * P], cw_st[:, t, :], ident[:])
            last.then_inc(cw_turned, 1)
            pe.wait_ge(on_done, g + 1)
            for c in range(DC):
                for t in range(GT):
                    last = nc.tensor.transpose(ps_h[0][:, c, t * P:(t + 1) * P], on[:, t, c * P:(c + 1) * P],
                                               ident[:])
            last.then_inc(o_turned, 1)

        def hidden(g, e, first):
            s = g * NX + e
            if first:
                pe.wait_ge(raw_lo, e + 1)
            if not (first and e < 2):
                pe.wait_ge(hid_done, s - 1)
            for i in range(2):
                k = 0
                for c in range(DC):
                    for w, xt in ((w13_hi, xT_hi), (w13_lo, xT_hi), (w13_hi, xT_lo)):
                        k += 1
                        last = nc.tensor.matmul(ps_h[e % 2][:, i, :], w[:, e, i, c, :],
                                                xt[:, c, bass.ds(g * GRP, GRP)], start=(k == 1), stop=(k == 3 * DC))
            last.then_inc(h_ready, 1)
            if e < E:
                nc.tensor.matmul(ps_c[:, e % 2, :], pick[:, e:e + 1].broadcast_to([2 * E, P]), cwT[:], start=True, stop=True).then_inc(c_ready, 1)

        def out_product(g, e):
            s = g * NX + e
            pe.wait_ge(hid_done, s + 1)
            for t in range(GT):
                last = nc.tensor.matmul(ps_y[:, t, :], hid[:, e % 2, t * P:(t + 1) * P], w2[:, e, :],
                                        start=False, stop=(e == NX - 1), skip_group_check=True)
            last.then_inc(y_part, 1)

        def attention_product(g):
            pe.wait_ge(oT_done, g + 1)
            pe.wait_ge(res_done, g)
            for t in range(GT):
                for c in range(DC):
                    nc.tensor.matmul(ps_y[:, t, :], oT[:, c, t * P:(t + 1) * P], wo[:, c, :],
                                     start=(t % 2 == 0 and c == 0), stop=False, skip_group_check=True)

        def group(g, first=False):
            turn(g)
            pe.wait_ge(cwT_done, g + 1)
            attention_product(g)
            hidden(g, 0, first)
            for e in range(NX):
                if e + 1 < NX:
                    hidden(g, e + 1, first)
                out_product(g, e)

        pe.wait_ge(w2_loaded, 48)
        pe.wait_ge(pick_2, 1)
        group(0, first=True)
        with pe.Fori(1, NG) as g:
            group(g)


_INS = ["L0_attn_x", "L0_attn_l_q1", "L0_attn_l_k1", "L0_attn_l_q2", "L0_attn_l_k2", "L0_attn_wq", "L0_attn_wk",
        "L0_attn_wv", "L0_attn_wo", "L0_ffn_w_router", "L0_ffn_we1", "L0_ffn_we3", "L0_ffn_we2", "L0_ffn_ws1",
        "L0_ffn_ws3", "L0_ffn_ws2"]
_TURNED = {"L0_attn_wq", "L0_attn_wk", "L0_attn_wv", "L0_attn_wo"}


def kernel(**inputs):
    import numpy as _np
    import concourse.bacc as _bacc
    from concourse import mybir as _mybir
    from concourse.bass_utils import run_bass_kernel_spmd as _run

    nc = _bacc.Bacc("TRN2", target_bir_lowering=False, num_devices=1)
    arrays, args = {}, []
    for name in _INS:
        a = _np.asarray(inputs[name])
        a = _np.ascontiguousarray(a.T if name in _TURNED else a)
        arrays[f"in_{name}"] = a
        args.append(nc.dram_tensor(f"in_{name}", a.shape, _mybir.dt.from_np(a.dtype), kind="ExternalInput").ap())
    out = nc.dram_tensor("out_0", (B, S, D), _mybir.dt.float32, kind="ExternalOutput").ap()
    o_dram = nc.dram_tensor("attention_out", (T, D), _mybir.dt.float32, kind="Internal").ap()
    build(nc, *args, out, o_dram)
    r = _run(nc, [arrays], core_ids=[0])
    return r.results[0]["out_0"]
```

```python
from contextlib import ExitStack
import math

import concourse.bass as bass
from concourse import mybir

F32 = mybir.dt.float32
F32R = mybir.dt.float32r
BF16 = mybir.dt.bfloat16
ALU = mybir.AluOpType
ACT = mybir.ActivationFunctionType
AX_X = mybir.AxisListType.X

P = 128
B, S, D = 4, 1024, 256
T = B * S
DC = D // P
NH = 8
DH = D // NH
NPAIR = B * NH
QB = S // P
GRP = 512
NG = T // GRP
GT = GRP // P
E, TOP_K, H, HS = 16, 4, 128, 512
NX = E + HS // H
WCOL = 2 * DC * H + D
WB = 4
NORM_G = DH // NH
L_INIT = 0.8 - 0.6 * math.exp(-0.3 * 1)
RMS_EPS = 1e-6
LN_EPS = 1e-5
SCALE = 1.0 / math.sqrt(DH)
MASKED = -1e30
NP = 4
STK = 3 * DH
NSTEP = 2 * QB
PARTS = [(h, i, k, min(k + GRP, (i + 1) * P)) for h in range(2) for i in range(QB)
         for k in range(0, (i + 1) * P, GRP)]
NPART = len(PARTS)
SIDE = {1: (0, 0, 0, 2), 2: (1, 1, 1, 2), 3: (1, 1, 1, 2), 4: (1, 1, 2, 2), 5: (1, 1, 0, 2), 6: (1, 1, 0, 0)}
WIDE_FROM = sum(sum(SIDE.get(c, ())) for c in range(QB // 2))
SPLIT_AT = 8
NB = 3


def wait(eng, sem, count):
    if not isinstance(count, int) or count > 0:
        eng.wait_ge(sem, count)


def build(nc, x, lq1, lk1, lq2, lk2, wqk, wvT, woT, wr, we1, we3, we2, ws1, ws3, ws2, out, o_dram, xT_dram):
    with ExitStack() as whole:
        keep = lambda n, s, d=F32: whole.enter_context(nc.sbuf_tensor(n, s, d))
        sem = lambda n: whole.enter_context(nc.semaphore(n))

        NW = NX * WCOL + DC * D
        with nc.sbuf_tensor("w_raw_all", [P, NW], F32) as w_raw_all:
            pass
        with nc.sbuf_tensor("w_lo_all", [P, NW], F32R) as w_lo_all:
            pass
        xT = keep("xT", [P, 2, DC, T], F32R)
        xT_hi, xT_lo = xT[:, 0], xT[:, 1]
        blocks = lambda a: (a[:, 0:NX * WCOL].rearrange("p (e n) -> p e n", n=WCOL),
                            a[:, NX * WCOL:NW].rearrange("p (c n) -> p c n", n=D))
        (w_raw, wo_raw), (w_lo, wo_lo) = blocks(w_raw_all), blocks(w_lo_all)
        raw_loaded = [sem(f"raw_loaded{i}") for i in range(NX // WB)]
        wo_loaded = sem("wo_loaded")
        cw_hl = keep("cw_hl", [P, T // P, 2 * E])
        gate = keep("gate", [P, T // P, E])
        ident = keep("ident", [P, P])
        neg_lam = keep("neg_lam", [P, 1])
        rms_eps = keep("rms_eps", [P, 1])
        x_tiles = x.rearrange("b (g t p) d -> (b g) p t d", p=P, t=GT)
        out_tiles = out.rearrange("b (g t p) d -> (b g) p t d", p=P, t=GT)

        with ExitStack() as early:
            v_all = early.enter_context(nc.sbuf_tensor("v_all", [P, T // P, D], F32))
            scores_r = early.enter_context(nc.sbuf_tensor("scores_r", [P, T // P, E], F32))
            with ExitStack() as ctx:
                project_tokens(nc, ctx, x_tiles, (lq1, lk1, lq2, lk2), wvT, wr, xT_hi, xT_lo, v_all, scores_r, gate, ident,
                               neg_lam, rms_eps)
            with ExitStack() as ctx:
                attention(nc, ctx, wqk, xT, xT_dram, v_all, scores_r, gate, cw_hl, ident, neg_lam, o_dram,
                          (woT, we1, we3, we2, ws1, ws3, ws2), w_raw, wo_raw, raw_loaded, wo_loaded)
        with ExitStack() as ctx:
            feed_forward(nc, ctx, x_tiles, out_tiles, o_dram, xT_dram, w_raw, wo_raw, w_lo, wo_lo, raw_loaded,
                         wo_loaded, cw_hl, ident, rms_eps)


def project_tokens(nc, ctx, x_tiles, lams, wvT, wr, xT_hi, xT_lo, v_all, scores_r, gate, ident, neg_lam, rms_eps):
    sb = lambda n, s, d=F32: ctx.enter_context(nc.sbuf_tensor(n, s, d))
    sem = lambda n: ctx.enter_context(nc.semaphore(n))
    NV = D + E
    x_in = sb("x_in", [P, 2, GT, D])
    xn = sb("xn", [P, 2, GT, D])
    stats = sb("stats", [P, 2, GT, 6])
    mean_var = sb("mean_var", [P, 2, GT, 2])
    std = sb("std", [P, 2, GT])
    rstd = sb("rstd", [P, 2, GT])
    st_hi = sb("st_hi", [P, 2, DC, GRP], F32R)
    st_lo = sb("st_lo", [P, 2, DC, GRP], F32R)
    wv_raw = sb("wv_raw", [P, DC, NV])
    wv_hi = sb("wv_hi", [P, DC, NV], F32R)
    wv_lo = sb("wv_lo", [P, DC, NV], F32R)
    lam_in = sb("lam_in", [P, 4, NH])
    lam_prod = sb("lam_prod", [P, 2, NH])
    lam_sum = sb("lam_sum", [P, 2])
    lam_exp = sb("lam_exp", [P, 2])
    ln_eps = sb("ln_eps", [P, 1])
    top = sb("top", [P, T // P])
    shifted = sb("shifted", [P, T // P, E])
    ps_t = [ctx.enter_context(nc.psum_tensor(f"ps_t{i}", [P, DC, GRP], F32)) for i in range(2)]
    ps_v = ctx.enter_context(nc.psum_tensor("ps_v", [P, GT, 512], F32))

    x_loaded = [sem(f"x_loaded{i}") for i in range(2)]
    wv_loaded, lam_loaded = sem("wv_loaded"), sem("lam_loaded")
    zeroed, consts, ident_made = sem("zeroed"), sem("consts"), sem("ident_made")
    wv_rounded, wv_split = sem("wv_rounded"), sem("wv_split")
    bn_done, stats_done, std_done, rstd_done, xn_done = (sem(n) for n in (
        "bn_done", "stats_done", "std_done", "rstd_done", "xn_done"))
    xt_in_psum, hi_done, lo_done, v_in_psum, v_copied, r_copied = (sem(n) for n in (
        "xt_in_psum", "hi_done", "lo_done", "v_in_psum", "v_copied", "r_copied"))
    kept = [sem(f"kept{i}") for i in range(2)]
    lam_a, lam_b, lam_c, lam_d = (sem(n) for n in ("lam_a", "lam_b", "lam_c", "lam_d"))
    top_done, shift_done, gate_done = (sem(n) for n in ("top_done", "shift_done", "gate_done"))

    block = ctx.enter_context(nc.Block())

    @block.sync
    def _(sp):
        sp.dma_start(wv_raw[:, :, 0:D], wvT.rearrange("(c p) n -> p c n", p=P)).then_inc(wv_loaded, 16)
        sp.dma_start(wv_raw[:, :, D:NV], wr.rearrange("(c p) n -> p c n", p=P)).then_inc(wv_loaded, 16)
        for i, lam in enumerate(lams):
            sp.dma_start(lam_in[:, i, :], lam.partition_broadcast(P)).then_inc(lam_loaded, 16)
        for g in range(2):
            sp.dma_start(x_in[:, g], x_tiles[g]).then_inc(x_loaded[g], 16)
        with sp.Fori(0, NG // 2) as trip:
            g0 = trip * 2
            for p in range(2):
                sp.wait_ge(lo_done, g0 + p + 1)
                cols = bass.ds((g0 + p) * GRP, GRP)
                sp.dma_start(xT_hi[:, :, cols].bitcast(F32), st_hi[:, p].bitcast(F32)).then_inc(kept[p], 16)
                sp.dma_start(xT_lo[:, :, cols].bitcast(F32), st_lo[:, p].bitcast(F32)).then_inc(kept[p], 16)
                sp.wait_ge(xn_done, g0 + p + 1)
                sp.dma_start(x_in[:, p], x_tiles[bass.ds((g0 + p + 2) % NG, 1)].rearrange("g p t d -> (g p) t d")
                             ).then_inc(x_loaded[p], 16)
        for p in range(2):
            sp.wait_ge(kept[p], 16 * NG)
            sp.wait_ge(x_loaded[p], 16 * (NG // 2 + 1))

    @block.gpsimd
    def _(pool):
        pool.memset(ident[:], 0.0).then_inc(zeroed, 1)
        pool.wait_ge(zeroed, 1)
        pool.affine_select(out=ident[:], in_=ident[:], compare_op=ALU.not_equal, fill=1.0, base=0,
                           pattern=[[-1, P]], channel_multiplier=1).then_inc(ident_made, 1)

    @block.vector
    def _(dve):
        nc.vector.memset(ln_eps[:], LN_EPS).then_inc(consts, 1)
        nc.vector.memset(rms_eps[:], RMS_EPS).then_inc(consts, 1)
        dve.wait_ge(wv_rounded, 1)
        nc.vector.tensor_tensor(wv_lo[:], wv_raw[:], wv_hi[:].bitcast(F32), ALU.subtract).then_inc(wv_split, 1)
        dve.wait_ge(lam_loaded, 64)
        nc.vector.tensor_tensor(lam_prod[:], lam_in[:, 0::2, :], lam_in[:, 1::2, :], ALU.mult).then_inc(lam_a, 1)
        dve.wait_ge(lam_a, 1)
        nc.vector.tensor_reduce(lam_sum[:], lam_prod[:], AX_X, ALU.add).then_inc(lam_b, 1)
        dve.wait_ge(lam_c, 1)
        nc.vector.tensor_tensor(neg_lam[:], lam_exp[:, 1:2], lam_exp[:, 0:1], ALU.subtract).then_inc(lam_d, 1)
        dve.wait_ge(lam_d, 1)
        nc.vector.tensor_scalar(neg_lam[:], neg_lam[:], -L_INIT, None, ALU.add).then_inc(lam_d, 1)

        def token_stats(g0, p):
            dve.wait_ge(x_loaded[p], g0 * 8 + 16)
            if p:
                dve.wait_ge(bn_done, g0 + p)
            for t in range(GT):
                last = nc.vector.bn_stats(stats[:, p, t, :], x_in[:, p, t, :])
            last.then_inc(bn_done, 1)

        def combine_stats(p):
            for t in range(GT):
                last = nc.vector.bn_aggr(mean_var[:, p, t, :], stats[:, p, t, :])
            last.then_inc(stats_done, 1)

        def invert_std(g0, p):
            if p == 0:
                dve.wait_ge(bn_done, g0 + 2)
            dve.wait_ge(std_done, g0 + p + 1)
            nc.vector.reciprocal(rstd[:, p], std[:, p]).then_inc(rstd_done, 1)

        def normalise(g0, p):
            dve.wait_ge(rstd_done, g0 + p + 1)
            dve.wait_ge(xt_in_psum, g0)
            for t in range(GT):
                last = nc.vector.tensor_scalar(xn[:, p, t, :], x_in[:, p, t, :], mean_var[:, p, t, 0:1],
                                               rstd[:, p, t:t + 1], ALU.subtract, ALU.mult)
            last.then_inc(xn_done, 1)

        def low_part(g, p):
            dve.wait_ge(hi_done, g + 1)
            nc.vector.tensor_tensor(st_lo[:, p], ps_t[p][:], st_hi[:, p].bitcast(F32), ALU.subtract
                                    ).then_inc(lo_done, 1)

        def router_out(g):
            dve.wait_ge(v_in_psum, g + 1)
            dve.wait_ge(v_copied, g + 1)
            nc.vector.tensor_copy(scores_r[:, bass.ds(g * GT, GT), :], ps_v[:, :, D:NV]).then_inc(r_copied, 1)

        with dve.Fori(0, NG // 2) as trip:
            g0 = trip * 2
            token_stats(g0, 0)
            token_stats(g0, 1)
            combine_stats(0)
            invert_std(g0, 0)
            combine_stats(1)
            normalise(g0, 0)
            invert_std(g0, 1)
            normalise(g0, 1)
            for p in range(2):
                low_part(g0 + p, p)
            for p in range(2):
                router_out(g0 + p)
        dve.wait_ge(r_copied, NG)
        nc.vector.tensor_reduce(top[:], scores_r[:], AX_X, ALU.max).then_inc(top_done, 1)
        dve.wait_ge(top_done, 1)
        nc.vector.tensor_tensor(shifted[:], scores_r[:], top[:].unsqueeze(2).broadcast_to([P, T // P, E]),
                                ALU.subtract).then_inc(shift_done, 1)

    @block.scalar
    def _(act):
        act.wait_ge(wv_loaded, 32)
        nc.scalar.activation(wv_hi[:], wv_raw[:], ACT.Copy).then_inc(wv_rounded, 1)
        act.wait_ge(lam_b, 1)
        nc.scalar.activation(lam_exp[:], lam_sum[:], ACT.Exp).then_inc(lam_c, 1)
        act.wait_ge(consts, 2)
        with act.Fori(0, NG // 2) as trip:
            g0 = trip * 2
            for p in range(2):
                act.wait_ge(stats_done, g0 + p + 1)
                nc.scalar.activation(std[:, p], mean_var[:, p, :, 1], ACT.Sqrt, bias=ln_eps[:]).then_inc(std_done, 1)
            for p in range(2):
                act.wait_ge(xt_in_psum, g0 + p + 1)
                act.wait_ge(kept[p], g0 * 16)
                nc.scalar.activation(st_hi[:, p], ps_t[p][:], ACT.Copy).then_inc(hi_done, 1)
            for p in range(2):
                act.wait_ge(v_in_psum, g0 + p + 1)
                nc.scalar.activation(v_all[:, bass.ds((g0 + p) * GT, GT), :], ps_v[:, :, 0:D], ACT.Copy
                                     ).then_inc(v_copied, 1)
        act.wait_ge(shift_done, 1)
        nc.scalar.activation(gate[:], shifted[:], ACT.Exp).then_inc(gate_done, 1)

    @block.tensor
    def _(pe):
        pe.wait_ge(ident_made, 1)

        def transposes(g, p):
            pe.wait_ge(xn_done, g + 1)
            pe.wait_ge(lo_done, g - p)
            for c in range(DC):
                for t in range(GT):
                    last = nc.tensor.transpose(ps_t[p][:, c, t * P:(t + 1) * P], xn[:, p, t, c * P:(c + 1) * P],
                                               ident[:])
            last.then_inc(xt_in_psum, 1)

        def values(g, p):
            pe.wait_ge(lo_done, g + 1)
            pe.wait_ge(v_copied, g)
            pe.wait_ge(r_copied, g)
            for t in range(GT):
                cols = slice(t * P, (t + 1) * P)
                n = 0
                for c in range(DC):
                    for a, b in ((st_hi, wv_hi), (st_hi, wv_lo), (st_lo, wv_hi)):
                        n += 1
                        last = nc.tensor.matmul(ps_v[:, t, 0:NV], a[:, p, c, cols], b[:, c, :],
                                                start=(n == 1), stop=(n == 3 * DC))
            last.then_inc(v_in_psum, 1)

        first = True
        with pe.Fori(0, NG // 2) as trip:
            g0 = trip * 2
            for p in range(2):
                transposes(g0 + p, p)
            if first:
                pe.wait_ge(wv_split, 1)
                first = False
            for p in range(2):
                values(g0 + p, p)


def attention(nc, ctx, wqk, xT, xT_dram, v_all, scores_r, gate, cw_hl, ident, neg_lam, o_dram, late_weights,
              w_late, wo_late, raw_loaded, wo_loaded):
    sb = lambda n, s, d=F32: ctx.enter_context(nc.sbuf_tensor(n, s, d))
    sem = lambda n: ctx.enter_context(nc.semaphore(n))
    xT_hi, xT_lo = xT[:, 0], xT[:, 1]
    w_raw = sb("w_raw", [P, DC, P])
    w_hi = sb("w_hi", [P, DC, P], F32R)
    w_lo = sb("w_lo", [P, DC, P], F32R)
    qk_hi = sb("qk_hi", [P, S], F32R)
    qk_lo = sb("qk_lo", [P, S], F32R)
    stack = sb("stack", [P, NB, 4, S], F32R)
    v_ones = sb("v_ones", [P, NB, QB, 2 * DH])
    probs = sb("probs", [P, NP, S])
    part_max = sb("part_max", [P, NB, 2 * QB, 2])
    row_max = sb("row_max", [P, NB, 2 * QB])
    max_row = sb("max_row", [2 * QB, P], F32R)
    o_raw = sb("o_raw", [P, S])
    rden = sb("rden", [P, QB, 2])
    rlam = sb("rlam", [P, QB])
    o_a = sb("o_a", [P, QB, DH])
    o_b = sb("o_b", [P, QB, DH])
    o_pair = sb("o_pair", [P, NB, QB, DH])
    mask = sb("mask", [P, GRP])
    masked_part = sb("masked_part", [P, 4, GRP], BF16)
    rank = sb("rank", [P, T // P, E])
    beats = sb("beats", [P, T // P, E])
    gate_sum = sb("gate_sum", [P, T // P])
    gate_inv = sb("gate_inv", [P, T // P])
    ps_s = [ctx.enter_context(nc.psum_tensor(f"ps_s{i}", [P, S], F32)) for i in range(2)]
    ps_x = ctx.enter_context(nc.psum_tensor("ps_x", [P, S], F32))
    ps_o = ctx.enter_context(nc.psum_tensor("ps_o", [P, S], F32))

    w_loaded, w_rounded, w_split = sem("w_loaded"), sem("w_rounded"), sem("w_split")
    mask_0, mask_1, ones_a, ones_b = (sem(n) for n in ("mask_0", "mask_1", "ones_a", "ones_b"))
    projected, hi_out, lo_out, stacked = (sem(n) for n in ("projected", "hi_out", "lo_out", "stacked"))
    side_scores, side_max, max_joined, max_filled, max_in_psum, max_turned, max_placed = (sem(n) for n in (
        "side_scores", "side_max", "max_joined", "max_filled", "max_in_psum", "max_turned", "max_placed"))
    scored, exped, cut, pv_done, v_staged = (sem(n) for n in ("scored", "exped", "cut", "pv_done", "v_staged"))
    o_copied, o_turned, rden_done, rlam_done, oa_done, ob_done, o_done = (sem(n) for n in (
        "o_copied", "o_turned", "rden_done", "rlam_done", "oa_done", "ob_done", "o_done"))
    o_free = [sem(f"o_free{i}") for i in range(NB)]
    ranked, v_filled, tokens_saved = sem("ranked"), sem("v_filled"), sem("tokens_saved")
    part_seen, exp_seen = sem("part_seen"), sem("exp_seen")

    Q, K = (0, 1), (2, 3)
    o_view = o_dram.rearrange("(b i p) d -> b p i d", p=P, i=QB)

    def part_bank(n, m):
        if m < WIDE_FROM or (isinstance(n, int) and n == 0):
            return ps_x[:, (m % 2) * GRP:(m % 2 + 1) * GRP]
        slot = (m - WIDE_FROM) % 4
        return ps_x[:, slot * GRP:(slot + 1) * GRP] if slot < 2 else ps_s[slot - 2][:, 0:GRP]

    def had_bank(n, m):
        if m < WIDE_FROM + 2 or (isinstance(n, int) and n == 0):
            return m - 2
        return m - 4 if m >= WIDE_FROM + 4 else -1

    block = ctx.enter_context(nc.Block())
    TRIPS = (NPAIR - 5) // NB

    @block.sync
    def _(sp):
        def load_weights(n):
            src = wqk[bass.ds(n % NH, 1)].rearrange("j (c p) m -> (j p) c m", p=P)
            wait(sp, w_split, n)
            sp.dma_start(w_raw[:], src).then_inc(w_loaded, 16)

        def stack_pair(n, p):
            sp.wait_ge(lo_out, 2 * (n + 1))
            for h in range(2):
                q, k = h * DH, (2 + h) * DH
                for src, row, place, at in ((qk_hi, q, Q[h], 0), (qk_lo, q, Q[h], DH), (qk_hi, q, Q[h], 2 * DH),
                                            (qk_hi, k, K[h], 0), (qk_hi, k, K[h], DH), (qk_lo, k, K[h], 2 * DH)):
                    sp.dma_start(stack[at:at + DH, p, place, :].bitcast(F32),
                                 src[row:row + DH, :].bitcast(F32)).then_inc(stacked, 16)

        def place_max(n, p):
            sp.wait_ge(max_turned, n + 1)
            sp.dma_start(stack[STK:STK + 1, p, 0:2, :].rearrange("r h s -> r (h s)").bitcast(F32),
                         max_row[:].bitcast(F32)).then_inc(max_placed, 16)

        def store(n, p):
            dst = o_view[bass.ds(n // NH, 1), :, :, bass.ds((n % NH) * DH, DH)].rearrange("b p i d -> (b p) i d")
            sp.wait_ge(o_done, n + 1)
            sp.dma_start(dst, o_pair[:, p]).then_inc(o_free[p], 16)

        def save_tokens(t):
            dst = xT_dram[bass.ds(t // GT, 1), :, :, :, bass.ds((t % GT) * P, P)]
            sp.dma_start(dst.rearrange("g p a c t -> (g p) a c t"),
                         xT[:, :, :, bass.ds(t * P, P)].bitcast(F32)).then_inc(tokens_saved, 16)

        def load_late(b):
            woT, we1, we3, we2, ws1, ws3, ws2 = late_weights
            dst = w_late[:, b * WB:(b + 1) * WB, :]
            for i, (w, ws) in enumerate(((we1, ws1), (we3, ws3))):
                for c in range(DC):
                    rows = slice(c * P, (c + 1) * P)
                    src = (w[b * WB:(b + 1) * WB, rows, :].rearrange("e p h -> p e h") if b * WB < E
                           else ws[rows, :].rearrange("p (e h) -> p e h", h=H))
                    at = (i * DC + c) * H
                    sp.dma_start(dst[:, :, at:at + H], src).then_inc(raw_loaded[b], 16)
            src = (we2[b * WB:(b + 1) * WB].rearrange("e h d -> h e d") if b * WB < E
                   else ws2.rearrange("(e h) d -> h e d", h=H))
            sp.dma_start(dst[:, :, 2 * DC * H:WCOL], src).then_inc(raw_loaded[b], 16)

        def step(n, p, stack_next=True, place=True, weights=True, stores=True, saves=True):
            if stack_next:
                stack_pair(n + 2, (p + 2) % NB)
            if saves:
                save_tokens(n + NB)
            if stores:
                store(n - 1, (p - 1) % NB)
            if weights:
                load_weights(n + 4)
            if place:
                place_max(n + 1, (p + 1) % NB)

        load_weights(0)
        load_weights(1)
        for t in range(NB):
            save_tokens(t)
        stack_pair(0, 0)
        load_weights(2)
        place_max(0, 0)
        stack_pair(1, 1)
        load_weights(3)
        step(0, 0, stores=False)
        with sp.Fori(0, TRIPS) as trip:
            for i in range(NB):
                step(trip * NB + (1 + i), (1 + i) % NB)
        n = TRIPS * NB + 1
        step(n, n % NB, weights=False)
        step(n + 1, (n + 1) % NB, weights=False, saves=False)
        sp.wait_ge(tokens_saved, 16 * (T // P))
        load_late(0)
        load_late(1)
        step(n + 2, (n + 2) % NB, stack_next=False, weights=False, saves=False)
        load_late(2)
        sp.dma_start(wo_late, late_weights[0].rearrange("(c p) n -> p c n", p=P)).then_inc(wo_loaded, 16)
        load_late(3)
        load_late(4)
        step(n + 3, (n + 3) % NB, stack_next=False, weights=False, place=False, saves=False)
        store(NPAIR - 1, (NPAIR - 1) % NB)
        for p in range(NB):
            sp.wait_ge(o_free[p], 16 * (1 + (NPAIR - 1 - p) // NB + 1))

    @block.gpsimd
    def _(pool):
        pool.memset(mask[:], 0.0).then_inc(mask_0, 1)
        pool.wait_ge(mask_0, 1)
        pool.affine_select(out=mask[:, GRP - P:GRP], in_=mask[:, GRP - P:GRP], compare_op=ALU.is_ge, fill=MASKED, base=0,
                           pattern=[[-1, P]], channel_multiplier=1).then_inc(mask_1, 1)
        pool.memset(v_ones[:], 1.0).then_inc(v_filled, 1)
        pool.wait_ge(v_filled, 1)

        for p in range(NB):
            pool.memset(o_pair[:, p], 0.0).then_inc(o_free[p], 16)

        def stage_values(n, p):
            if not isinstance(n, int) or n >= NB:
                pool.wait_ge(pv_done, QB * (n - NB + 1))
            pool.tensor_copy(v_ones[:, p, :, 0:DH],
                             v_all[:, bass.ds((n // NH) * QB, QB), bass.ds((n % NH) * DH, DH)]).then_inc(v_staged, 1)

        def cut_diagonal(n, c, h):
            at = (2 * c + h) % NP
            pool.wait_ge(exped, NSTEP * n + 2 * c + h + 1)
            pool.sem_inc(exp_seen, 1)
            pool.affine_select(out=probs[:, at, c * P:(c + 1) * P], in_=probs[:, at, c * P:(c + 1) * P],
                               compare_op=ALU.is_ge, fill=0.0, base=0, pattern=[[1, P]], channel_multiplier=-1
                               ).then_inc(cut, 1)

        def step(n, p, stages=True):
            for c in range(QB):
                for h in range(2):
                    cut_diagonal(n, c, h)
                if c == 1 and stages:
                    stage_values(n + 2, (p + 2) % NB)

        for n in range(2):
            stage_values(n, n)
        step(0, 0)
        with pool.Fori(0, TRIPS) as trip:
            for i in range(NB):
                step(trip * NB + (1 + i), (1 + i) % NB)
        for n in range(TRIPS * NB + 1, NPAIR):
            step(n, n % NB, stages=n + 2 < NPAIR)

    @block.tensor
    def _(pe):
        def project(n, half):
            pe.wait_ge(w_split, n + 1)
            if half == 1:
                wait(pe, max_turned, min(n, 1) if isinstance(n, int) and n < NB else n - 1)
            elif isinstance(n, int) and n < NB:
                wait(pe, lo_out, 2 * n)
                wait(pe, side_max, NPART * min(n, 1))
            else:
                pe.wait_ge(side_max, NPART * (n - 1))
            col = (n // NH) * S + half * GRP
            k = 0
            for c in range(DC):
                for w, xt in ((w_hi, xT_hi), (w_lo, xT_hi), (w_hi, xT_lo)):
                    k += 1
                    last = nc.tensor.matmul(ps_x[:, half * GRP:(half + 1) * GRP], w[:, c, :],
                                            xt[:, c, bass.ds(col, GRP)], start=(k == 1), stop=(k == 3 * DC))
            last.then_inc(projected, 1)

        def side(n, p, m):
            h, i, k0, k1 = PARTS[m]
            if m == 0:
                pe.wait_ge(stacked, 192 * (n + 1))
            before = had_bank(n, m)
            if before >= 0:
                pe.wait_ge(side_max, NPART * n + before + 1)
            last = nc.tensor.matmul(part_bank(n, m)[:, 0:k1 - k0], stack[0:STK, p, Q[h], i * P:(i + 1) * P],
                                    stack[0:STK, p, K[h], k0:k1], start=True, stop=True)
            last.then_inc(side_scores, 1)

        def turn_max(n, p):
            pe.wait_ge(max_joined, n + 1)
            nc.tensor.transpose(ps_x[0:2 * QB, GRP:GRP + P], row_max[:, p, :], ident[:]).then_inc(max_in_psum, 1)

        def score(n, p, c, h):
            s = 2 * c + h
            if s == 0:
                pe.wait_ge(max_placed, 16 * (n + 1))
            if not (isinstance(n, int) and n == 0 and s < 2):
                pe.wait_ge(exped, NSTEP * n + s - 1)
            ps = ps_s[h]
            q0 = c * P
            while q0 < S:
                q1 = min((q0 // GRP + 1) * GRP, S)
                last = nc.tensor.matmul(ps[:, q0:q1], stack[0:STK + 1, p, K[h], c * P:(c + 1) * P],
                                        stack[0:STK + 1, p, Q[h], q0:q1], start=True, stop=True)
                q0 = q1
            last.then_inc(scored, 1)

        def value(n, p, c, bank):
            q0, q1 = max(c * P, bank * GRP), (bank + 1) * GRP
            if c == 0 and bank == 0:
                pe.wait_ge(v_staged, n + 1)
                wait(pe, o_copied, n)
            if q1 <= q0:
                return
            if q0 == c * P:
                pe.wait_ge(cut, NSTEP * n + 2 * c + 2)
            for h in range(2):
                last = nc.tensor.matmul(ps_o[h * 64:(h + 1) * 64, q0:q1], v_ones[:, p, c, :],
                                        probs[:, (2 * c + h) % NP, q0:q1], start=(c == 0),
                                        stop=(c * P + P >= q1))
            if bank == 1:
                last.then_inc(pv_done, 1)

        def turn_out(n):
            pe.wait_ge(o_copied, n + 1)
            if isinstance(n, int):
                wait(pe, ob_done, n)
            pe.wait_ge(lo_out, 2 * (n + 4) if not isinstance(n, int) else 2 * min(n + 4, NPAIR))
            for i in range(QB):
                last = nc.tensor.transpose(ps_x[:, i * P:(i + 1) * P], o_raw[:, i * P:(i + 1) * P], ident[:])
            last.then_inc(o_turned, 1)

        def step(n, p, sides=True, projects=True, turns=True):
            parts = iter(range(NPART) if sides else ())

            def some(count):
                for _, m in zip(range(count), parts):
                    side(n + 1, (p + 1) % NB, m)

            for c in range(QB):
                after = SIDE.get(c, (0, 0, 0, 0))
                for h in range(2):
                    score(n, p, c, h)
                    some(after[h])
                if c == 0 and turns:
                    turn_out(n - 1)
                if c > 0:
                    for bank in range(2):
                        value(n, p, c - 1, bank)
                        if c == 1 and bank == 1 and sides:
                            pe.wait_ge(ob_done, n) if turns else pe.wait_ge(lo_out, 2 * NB)
                        some(after[2 + bank])
            if sides:
                turn_max(n + 1, (p + 1) % NB)
            if projects:
                project(n + 3, 0)
            value(n, p, QB - 1, 1)
            if projects:
                project(n + 3, 1)

        pe.wait_ge(ones_b, 1)
        project(0, 0)
        project(0, 1)
        pe.wait_ge(lo_out, 2)
        for m in range(NPART):
            side(0, 0, m)
        turn_max(0, 0)
        for n in range(1, NB):
            project(n, 0)
            project(n, 1)
        step(0, 0, turns=False)
        with pe.Fori(0, TRIPS) as trip:
            for i in range(NB):
                step(trip * NB + (1 + i), (1 + i) % NB)
        n = TRIPS * NB + 1
        step(n, n % NB)
        step(n + 1, (n + 1) % NB, projects=False)
        step(n + 2, (n + 2) % NB, projects=False)
        step(n + 3, (n + 3) % NB, sides=False, projects=False)
        turn_out(NPAIR - 1)

    @block.scalar
    def _(act):
        def round_weights(n):
            act.wait_ge(w_loaded, 16 * (n + 1))
            wait(act, projected, 2 * n)
            nc.scalar.activation(w_hi[:], w_raw[:], ACT.Copy).then_inc(w_rounded, 1)

        def high_part(n, half):
            cols = slice(half * GRP, (half + 1) * GRP)
            act.wait_ge(projected, 2 * n + half + 1)
            if half == 0:
                wait(act, stacked, 192 * n)
            nc.scalar.activation(qk_hi[:, cols], ps_x[:, cols], ACT.Copy).then_inc(hi_out, 1)

        def copy_out(n):
            act.wait_ge(pv_done, QB * (n + 1))
            wait(act, o_turned, n)
            nc.scalar.activation(o_raw[:], ps_o[:], ACT.Copy).then_inc(o_copied, 1)

        def exp(n, c, h):
            s = 2 * c + h
            act.wait_ge(scored, NSTEP * n + s + 1)
            if not (isinstance(n, int) and n == 0 and s < NP):
                act.wait_ge(pv_done, QB * n + c - NP // 2 + 1)
            nc.scalar.activation(probs[:, s % NP, c * P:S], ps_s[h][:, c * P:S], ACT.Exp, scale=SCALE
                                 ).then_inc(exped, 1)

        def step(n, projects=True):
            for c in range(QB):
                for h in range(2):
                    exp(n, c, h)
                if projects and c == 1:
                    round_weights(n + 3)
            if projects:
                high_part(n + 3, 0)
            copy_out(n)
            if projects:
                high_part(n + 3, 1)

        round_weights(0)
        act.wait_ge(ones_a, 1)
        for p in range(NB):
            for h in range(2):
                last = nc.scalar.activation(stack[STK:STK + 1, p, K[h], :], o_raw[STK:STK + 1, :], ACT.Copy)
        last.then_inc(ones_b, 1)
        for n in range(NB):
            high_part(n, 0)
            high_part(n, 1)
            if n < NB - 1:
                round_weights(n + 1)
        step(0)
        with act.Fori(0, TRIPS) as trip:
            for i in range(NB):
                step(trip * NB + 1 + i)
        n = TRIPS * NB + 1
        step(n)
        for k in range(n + 1, NPAIR):
            step(k, projects=False)

    @block.vector
    def _(dve):
        def split_weights(n):
            dve.wait_ge(w_rounded, n + 1)
            nc.vector.tensor_tensor(w_lo[:], w_raw[:], w_hi[:].bitcast(F32), ALU.subtract).then_inc(w_split, 1)

        def low_part(n, half):
            cols = slice(half * GRP, (half + 1) * GRP)
            dve.wait_ge(hi_out, 2 * n + half + 1)
            nc.vector.tensor_tensor(qk_lo[:, cols], ps_x[:, cols], qk_hi[:, cols].bitcast(F32), ALU.subtract
                                    ).then_inc(lo_out, 1)

        def side_maxima(n, p, m):
            h, i, k0, k1 = PARTS[m]
            dve.wait_ge(side_scores, NPART * n + m + 1)
            if k1 == (i + 1) * P:
                dve.sem_inc(part_seen, 1)
            out, part, width = part_max[:, p, h * QB + i, k0 // GRP:k0 // GRP + 1], part_bank(n, m)[:, 0:k1 - k0], k1 - k0
            if k1 == (i + 1) * P:
                nc.vector.tensor_tensor_reduce(masked_part[:, m % 4, 0:width], part, mask[:, GRP - width:GRP], 1.0,
                                               -3e38, ALU.add, ALU.max, out).then_inc(side_max, 1)
            else:
                nc.vector.tensor_reduce(out, part, AX_X, ALU.max).then_inc(side_max, 1)

        def join_maxima(n, p):
            dve.wait_ge(side_max, NPART * (n + 1))
            nc.vector.tensor_reduce(row_max[:, p, :], part_max[:, p], AX_X, ALU.max).then_inc(max_joined, 1)

        def negate_max(n):
            dve.wait_ge(max_in_psum, n + 1)
            wait(dve, max_placed, 16 * n)
            nc.vector.tensor_scalar(max_row[:], ps_x[0:2 * QB, GRP:GRP + P], -1.0, None, ALU.mult).then_inc(max_turned, 1)

        def combine(n, p):
            turned = ps_x[:].rearrange("q (i f) -> q i f", f=P)
            dve.wait_ge(o_turned, n + 1)
            nc.vector.reciprocal(rden[:], turned[:, :, DH::2 * DH]).then_inc(rden_done, 1)
            dve.wait_ge(rden_done, n + 1)
            nc.vector.tensor_scalar(rlam[:], rden[:, :, 1], neg_lam[:, 0:1], None, ALU.mult).then_inc(rlam_done, 1)
            nc.vector.tensor_tensor(o_a[:], turned[:, :, 0:DH], rden[:, :, 0:1].broadcast_to([P, QB, DH]), ALU.mult
                                    ).then_inc(oa_done, 1)
            dve.wait_ge(rlam_done, n + 1)
            nc.vector.tensor_tensor(o_b[:], turned[:, :, 2 * DH:3 * DH],
                                    rlam[:].unsqueeze(2).broadcast_to([P, QB, DH]), ALU.mult).then_inc(ob_done, 1)
            dve.wait_ge(oa_done, n + 1)
            dve.wait_ge(ob_done, n + 1)
            dve.wait_ge(o_free[p], (n // NB) * 16 + 16)
            nc.vector.tensor_tensor(o_pair[:, p], o_a[:], o_b[:], ALU.add).then_inc(o_done, 1)

        def rank_by(f, add):
            dve.wait_ge(ranked, 2 * f + 1 + add)
            if add:
                nc.vector.tensor_tensor(rank[:], rank[:], beats[:], ALU.add).then_inc(ranked, 1)
                return
            for lo, hi, op in ((0, f + 1, ALU.is_gt), (f + 1, E, ALU.is_ge)):
                if hi > lo:
                    last = nc.vector.tensor_tensor(
                        beats[:, :, lo:hi], scores_r[:, :, f:f + 1].broadcast_to([P, T // P, hi - lo]),
                        scores_r[:, :, lo:hi], op)
            last.then_inc(ranked, 1)

        def routing_weights():
            dve.wait_ge(ranked, 2 * E + 1)
            nc.vector.scalar_tensor_tensor(out=gate[:], in0=rank[:], scalar=TOP_K - 0.5, in1=gate[:], op0=ALU.is_lt,
                                           op1=ALU.mult).then_inc(ranked, 1)
            dve.wait_ge(ranked, 2 * E + 2)
            nc.vector.tensor_reduce(gate_sum[:], gate[:], AX_X, ALU.add).then_inc(ranked, 1)
            dve.wait_ge(ranked, 2 * E + 3)
            nc.vector.reciprocal(gate_inv[:], gate_sum[:]).then_inc(ranked, 1)
            dve.wait_ge(ranked, 2 * E + 4)
            nc.vector.scalar_tensor_tensor(out=gate[:], in0=gate[:], scalar=TOP_K / (TOP_K + 1.0),
                                           in1=gate_inv[:].unsqueeze(2).broadcast_to([P, T // P, E]),
                                           op0=ALU.mult, op1=ALU.mult).then_inc(ranked, 1)
            dve.wait_ge(ranked, 2 * E + 5)
            nc.vector.tensor_copy(cw_hl[:, :, 0:E].bitcast(F32R), gate[:]).then_inc(ranked, 1)
            dve.wait_ge(ranked, 2 * E + 6)
            nc.vector.tensor_tensor(cw_hl[:, :, E:2 * E], gate[:], cw_hl[:, :, 0:E], ALU.subtract).then_inc(ranked, 1)

        def step(n, p, sides=True, projects=True, turns=True, ranks=None):
            if turns:
                combine(n - 1, (p - 1) % NB)
            if sides:
                for m in range(NPART):
                    side_maxima(n + 1, (p + 1) % NB, m)
                    if ranks is not None and m % 2 == 0 and ranks + m // 2 < 2 * E:
                        rank_by((ranks + m // 2) // 2, (ranks + m // 2) % 2)
                    if projects and m == SPLIT_AT:
                        split_weights(n + 3)
                join_maxima(n + 1, (p + 1) % NB)
                negate_max(n + 1)
            if projects:
                low_part(n + 3, 0)
                low_part(n + 3, 1)

        nc.vector.memset(o_raw[STK:STK + 1, :], 1.0).then_inc(ones_a, 1)
        nc.vector.memset(part_max[:], -3e38).then_inc(max_filled, 1)
        dve.wait_ge(max_filled, 1)
        dve.wait_ge(mask_1, 1)
        split_weights(0)
        low_part(0, 0)
        low_part(0, 1)
        split_weights(1)
        for m in range(NPART):
            side_maxima(0, 0, m)
        join_maxima(0, 0)
        negate_max(0)
        for n in range(1, NB):
            low_part(n, 0)
            low_part(n, 1)
            if n < NB - 1:
                split_weights(n + 1)
        step(0, 0, turns=False)
        with dve.Fori(0, TRIPS) as trip:
            for i in range(NB):
                step(trip * NB + (1 + i), (1 + i) % NB)
        n = TRIPS * NB + 1
        nc.vector.memset(rank[:], 0.0).then_inc(ranked, 1)
        step(n, n % NB, ranks=0)
        step(n + 1, (n + 1) % NB, projects=False, ranks=NPART // 2)
        step(n + 2, (n + 2) % NB, projects=False, ranks=NPART)
        routing_weights()
        step(n + 3, (n + 3) % NB, sides=False, projects=False)
        combine(NPAIR - 1, (NPAIR - 1) % NB)


def feed_forward(nc, ctx, x_tiles, out_tiles, o_dram, xT_dram, w_raw, wo_raw, w_lo, wo_lo, raw_loaded, wo_loaded,
                 cw_hl, ident, rms_eps):
    sb = lambda n, s, d=F32: ctx.enter_context(nc.sbuf_tensor(n, s, d))
    sem = lambda n: ctx.enter_context(nc.semaphore(n))
    w_hi = sb("we_hi", [P, NX, WCOL], F32R)
    wo_hi = sb("wo_hi", [P, DC, D], F32R)
    xg = sb("xg", [P, 2, 2, DC, GRP], F32R)
    pick_f = sb("pick_f", [2 * E, E])
    pick = sb("pick", [2 * E, E], F32R)
    cw_st = sb("cw_st", [P, GT, 2 * E])
    cwT = sb("cwT", [2 * E, GRP], F32R)
    o_in = sb("o_in", [P, GT, D])
    ms = sb("ms", [P, GT, D // NORM_G])
    on = sb("on", [P, GT, D])
    oT_hi = sb("oT_hi", [P, DC, GRP], F32R)
    oT_lo = sb("oT_lo", [P, DC, GRP], F32R)
    res = sb("res", [P, GT, D])
    act_h = sb("act_h", [P, 2, GRP])
    mid = sb("mid", [P, 2, GRP])
    hid = sb("hid", [P, 2, GRP])
    hid_hi = sb("hid_hi", [P, 2, GRP], F32R)
    hid_lo = sb("hid_lo", [P, 2, GRP], F32R)
    ps_h = [ctx.enter_context(nc.psum_tensor(f"ps_h{i}", [P, 2, GRP], F32)) for i in range(2)]
    ps_c = ctx.enter_context(nc.psum_tensor("ps_c", [P, 2, GRP], F32))
    ps_y = ctx.enter_context(nc.psum_tensor("ps_y", [P, GT, D], F32))

    w_rounded, w_split, wo_rounded, wo_split = (sem(n) for n in ("we_rounded", "we_split", "wo_rounded", "wo_split"))
    pick_0, pick_1, pick_2 = (sem(n) for n in ("pick_0", "pick_1", "pick_2"))
    cw_staged, cw_turned, cwT_done = (sem(n) for n in ("cw_staged", "cw_turned", "cwT_done"))
    o_loaded, x_loaded, xg_loaded, sq_done, ms_done, rms_done, rr_done, on_done, o_turned, oT_rounded, oT_split = (
        sem(n) for n in ("f_o_loaded", "f_x_loaded", "xg_loaded", "sq_done", "ms_done", "rms_done", "rr_done",
                         "on_done", "f_o_turned", "oT_rounded", "oT_split"))
    h_ready, c_ready, silu_done, mid_done, hid_done, hi_done, lo_done, y_part, res_done, stored = (sem(n) for n in (
        "h_ready", "c_ready", "silu_done", "mid_done", "hid_done", "f_hi_done", "f_lo_done", "y_part", "res_done",
        "stored"))
    o_tiles = o_dram.rearrange("(g t p) d -> g p t d", p=P, t=GT)
    one = lambda ap: ap.rearrange("g p t d -> (g p) t d")
    AT_SQUARE, AT_SUM, AT_ROOT, AT_SCALE, AT_TURN_O, AT_TURN_CW = 6, 7, 8, 9, E + 1, E + 3
    PAIRS = (NG - 2) // 2

    block = ctx.enter_context(nc.Block())

    @block.sync
    def _(sp):
        def load_tokens(g, p):
            sp.dma_start(xg[:, p].bitcast(F32), xT_dram[bass.ds(g, 1)].rearrange("g p a c t -> (g p) a c t")
                         ).then_inc(xg_loaded, 16)

        def group(g, p, last=False):
            if not last:
                sp.wait_ge(h_ready, g * NX + 1)
                load_tokens(g + 1, 1 - p)
                sp.wait_ge(on_done, g + 1)
                sp.dma_start(o_in[:], one(o_tiles[bass.ds(g + 1, 1)])).then_inc(o_loaded, 16)
            sp.wait_ge(res_done, g + 1)
            sp.dma_start(one(out_tiles[bass.ds(g, 1)]), res[:]).then_inc(stored, 16)
            if not last:
                sp.wait_ge(stored, 16 * (g + 1))
                sp.dma_start(res[:], one(x_tiles[bass.ds(g + 1, 1)])).then_inc(x_loaded, 16)

        load_tokens(0, 0)
        sp.dma_start(o_in[:], o_tiles[0]).then_inc(o_loaded, 16)
        sp.dma_start(res[:], x_tiles[0]).then_inc(x_loaded, 16)
        group(0, 0)
        with sp.Fori(0, PAIRS) as trip:
            for i in range(1, 3):
                group(trip * 2 + i, i % 2)
        group(NG - 1, 1, last=True)
        sp.wait_ge(stored, 16 * NG)

    @block.gpsimd
    def _(pool):
        pool.tensor_copy(cw_st[:], cw_hl[:, 0:GT, :]).then_inc(cw_staged, 1)
        pool.memset(pick_f[:], 0.0).then_inc(pick_0, 1)
        pool.wait_ge(pick_0, 1)
        for i in range(2):
            pool.affine_select(out=pick_f[:], in_=pick_f[:], compare_op=ALU.not_equal, fill=1.0, base=-E * i,
                               pattern=[[-1, E]], channel_multiplier=1).then_inc(pick_1, 1)
            pool.wait_ge(pick_1, i + 1)
        with pool.Fori(1, NG) as g:
            pool.wait_ge(cw_turned, g)
            pool.tensor_copy(cw_st[:], cw_hl[:, bass.ds(g * GT, GT), :]).then_inc(cw_staged, 1)

    @block.scalar
    def _(act):
        def round_weights(e):
            if e % WB == 0:
                act.wait_ge(raw_loaded[e // WB], 16 * (2 * DC + 1))
            nc.scalar.activation(w_hi[:, e], w_raw[:, e], ACT.Copy).then_inc(w_rounded, 1)

        def root(g):
            act.wait_ge(ms_done, g + 1)
            nc.scalar.activation(ms[:], ms[:], ACT.Sqrt, scale=1.0 / NORM_G, bias=rms_eps[:]).then_inc(rms_done, 1)

        def round_output(g, ps):
            act.wait_ge(o_turned, g + 1)
            nc.scalar.activation(oT_hi[:], ps, ACT.Copy).then_inc(oT_rounded, 1)

        def copy_routing(g):
            act.wait_ge(cw_turned, g + 1)
            nc.scalar.activation(cwT[:], ps_c[0:2 * E, 0, :], ACT.Copy).then_inc(cwT_done, 1)

        def expert(g, e, first):
            s = g * NX + e
            act.wait_ge(h_ready, s + 1)
            nc.scalar.activation(act_h[:, e % 2, :], ps_h[e % 2][:, 0, :], ACT.Silu).then_inc(silu_done, 1)
            act.wait_ge(hid_done, s + 1)
            if not (first and e < 2):
                act.wait_ge(y_part, s - 1)
            nc.scalar.activation(hid_hi[:, e % 2, :], hid[:, e % 2, :], ACT.Copy).then_inc(hi_done, 1)

        def group(g, first=False, last=False):
            for e in range(NX):
                expert(g, e, first)
                if first and e + 2 < NX:
                    round_weights(e + 2)
                if first and e == 1:
                    round_output(0, ps_y[:].rearrange("p t d -> p (t d)"))
                if not last:
                    if e == AT_ROOT:
                        root(g + 1)
                    if e == AT_TURN_O:
                        round_output(g + 1, ps_c[:].rearrange("p c t -> p (c t)"))
                    if e == AT_TURN_CW:
                        copy_routing(g + 1)

        round_weights(0)
        act.wait_ge(pick_1, 2)
        nc.scalar.activation(pick[:], pick_f[:], ACT.Copy).then_inc(pick_2, 1)
        copy_routing(0)
        round_weights(1)
        root(0)
        act.wait_ge(wo_loaded, 16)
        nc.scalar.activation(wo_hi[:], wo_raw, ACT.Copy).then_inc(wo_rounded, 1)
        group(0, first=True)
        with act.Fori(0, PAIRS) as trip:
            for i in range(1, 3):
                group(trip * 2 + i)
        group(NG - 1, last=True)

    @block.vector
    def _(dve):
        def split_weights(e):
            dve.wait_ge(w_rounded, e + 1)
            nc.vector.tensor_tensor(w_lo[:, e], w_raw[:, e], w_hi[:, e].bitcast(F32), ALU.subtract
                                    ).then_inc(w_split, 1)

        def square(g):
            dve.wait_ge(o_loaded, 16 * (g + 1))
            wait(dve, o_turned, g)
            nc.vector.tensor_tensor(on[:], o_in[:], o_in[:], ALU.mult).then_inc(sq_done, 1)

        def sum_squares(g):
            dve.wait_ge(sq_done, g + 1)
            wait(dve, on_done, g)
            nc.vector.tensor_reduce(ms[:], on[:].rearrange("p t (n k) -> p t n k", k=NORM_G), AX_X, ALU.add
                                    ).then_inc(ms_done, 1)

        def scale(g):
            dve.wait_ge(rms_done, g + 1)
            nc.vector.reciprocal(ms[:], ms[:]).then_inc(rr_done, 1)
            dve.wait_ge(rr_done, g + 1)
            nc.vector.scalar_tensor_tensor(
                out=on[:].rearrange("p t (n k) -> p (t n) k", k=NORM_G),
                in0=o_in[:].rearrange("p t (n k) -> p (t n) k", k=NORM_G), scalar=1.0 - L_INIT,
                in1=ms[:].rearrange("p t n -> p (t n)").unsqueeze(2).broadcast_to([P, GT * D // NORM_G, NORM_G]),
                op0=ALU.mult, op1=ALU.mult).then_inc(on_done, 1)

        def split_output(g, ps):
            dve.wait_ge(oT_rounded, g + 1)
            nc.vector.tensor_tensor(oT_lo[:].rearrange("p c t -> p (c t)"), ps,
                                    oT_hi[:].rearrange("p c t -> p (c t)").bitcast(F32), ALU.subtract
                                    ).then_inc(oT_split, 1)

        def expert(g, e, first):
            s = g * NX + e
            later = not (first and e < 2)
            dve.wait_ge(silu_done, s + 1)
            if later:
                dve.wait_ge(hid_done, s - 1)
            nc.vector.tensor_tensor(mid[:, e % 2, :], ps_h[e % 2][:, 1, :], act_h[:, e % 2, :], ALU.mult
                                    ).then_inc(mid_done, 1)
            dve.wait_ge(mid_done, s + 1)
            if later:
                dve.wait_ge(lo_done, s - 1)
            if e < E:
                dve.wait_ge(c_ready, g * E + e + 1)
                nc.vector.tensor_tensor(hid[:, e % 2, :], ps_c[:, e % 2, :], mid[:, e % 2, :], ALU.mult
                                        ).then_inc(hid_done, 1)
            else:
                nc.vector.tensor_scalar(hid[:, e % 2, :], mid[:, e % 2, :], 1.0 / (TOP_K + 1.0), None, ALU.mult
                                        ).then_inc(hid_done, 1)
            dve.wait_ge(hi_done, s + 1)
            nc.vector.tensor_tensor(hid_lo[:, e % 2, :], hid[:, e % 2, :], hid_hi[:, e % 2, :].bitcast(F32),
                                    ALU.subtract).then_inc(lo_done, 1)

        def residual(g):
            dve.wait_ge(x_loaded, 16 * (g + 1))
            dve.wait_ge(y_part, NX * (g + 1))
            nc.vector.tensor_tensor(res[:], ps_y[:], res[:], ALU.add).then_inc(res_done, 1)

        def group(g, first=False, last=False):
            for e in range(NX):
                expert(g, e, first)
                if first and e + 2 < NX:
                    split_weights(e + 2)
                if first and e == 1:
                    split_output(0, ps_y[:].rearrange("p t d -> p (t d)"))
                if e == 0 and not first:
                    residual(g - 1)
                if not last:
                    if e == AT_SQUARE:
                        square(g + 1)
                    if e == AT_SUM:
                        sum_squares(g + 1)
                    if e == AT_SCALE:
                        scale(g + 1)
                    if e == AT_TURN_O:
                        split_output(g + 1, ps_c[:].rearrange("p c t -> p (c t)"))

        split_weights(0)
        square(0)
        sum_squares(0)
        split_weights(1)
        scale(0)
        dve.wait_ge(wo_rounded, 1)
        nc.vector.tensor_tensor(wo_lo, wo_raw, wo_hi[:].bitcast(F32), ALU.subtract).then_inc(wo_split, 1)
        group(0, first=True)
        with dve.Fori(0, PAIRS) as trip:
            for i in range(1, 3):
                group(trip * 2 + i)
        group(NG - 1, last=True)
        residual(NG - 1)

    @block.tensor
    def _(pe):
        def turn_routing(g):
            pe.wait_ge(cw_staged, g + 1)
            if not (isinstance(g, int) and g == 0):
                pe.wait_ge(oT_split, g + 1)
            for t in range(GT):
                last = nc.tensor.transpose(ps_c[0:2 * E, 0, t * P:(t + 1) * P], cw_st[:, t, :], ident[:])
            last.then_inc(cw_turned, 1)

        def turn_output(g, ps):
            pe.wait_ge(on_done, g + 1)
            if not (isinstance(g, int) and g == 0):
                pe.wait_ge(hid_done, (g - 1) * NX + E)
            for c in range(DC):
                for t in range(GT):
                    at = c * GRP + t * P
                    last = nc.tensor.transpose(ps[:, at:at + P], on[:, t, c * P:(c + 1) * P], ident[:])
            last.then_inc(o_turned, 1)

        def hidden(g, p, e, first):
            s = g * NX + e
            if e == 0:
                pe.wait_ge(xg_loaded, 16 * (g + 1))
            if first:
                pe.wait_ge(w_split, e + 1)
            if not (first and e < 2):
                pe.wait_ge(mid_done, s - 1)
            for i in range(2):
                k = 0
                for c in range(DC):
                    at = (i * DC + c) * H
                    for w, a in ((w_hi, 0), (w_lo, 0), (w_hi, 1)):
                        k += 1
                        last = nc.tensor.matmul(ps_h[e % 2][:, i, :], w[:, e, at:at + H], xg[:, p, a, c, :],
                                                start=(k == 1), stop=(k == 3 * DC))
            last.then_inc(h_ready, 1)

        def spread_routing(g, e, first):
            if e == 0:
                pe.wait_ge(cwT_done, g + 1)
            if e >= 2:
                pe.wait_ge(hid_done, g * NX + e - 1)
            nc.tensor.matmul(ps_c[:, e % 2, :], pick[:, e:e + 1].broadcast_to([2 * E, P]), cwT[:], start=True,
                             stop=True).then_inc(c_ready, 1)

        def out_product(g, e):
            pe.wait_ge(lo_done, g * NX + e + 1)
            for t in range(GT):
                rows = slice(t * P, (t + 1) * P)
                for a, w in ((hid_hi, w_hi), (hid_hi, w_lo), (hid_lo, w_hi)):
                    last = nc.tensor.matmul(ps_y[:, t, :], a[:, e % 2, rows], w[:, e, 2 * DC * H:WCOL], start=False,
                                            stop=(e == NX - 1), skip_group_check=True)
            last.then_inc(y_part, 1)

        def attention_product(g):
            pe.wait_ge(oT_split, g + 1)
            if isinstance(g, int) and g == 0:
                pe.wait_ge(wo_split, 1)
            else:
                pe.wait_ge(res_done, g)
            for t in range(GT):
                rows = slice(t * P, (t + 1) * P)
                for c in range(DC):
                    for i, (a, w) in enumerate(((oT_hi, wo_hi), (oT_hi, wo_lo), (oT_lo, wo_hi))):
                        nc.tensor.matmul(ps_y[:, t, :], a[:, c, rows], w[:, c, :],
                                         start=(t % 2 == 0 and c == 0 and i == 0), stop=False, skip_group_check=True)

        def group(g, p, first=False, last=False):
            for e in range(NX):
                hidden(g, p, e, first)
                if e == 2:
                    attention_product(g)
                if e >= 2:
                    out_product(g, e - 2)
                elif not first:
                    out_product(g - 1, NX - 2 + e)
                if e < E:
                    spread_routing(g, e, first)
                if first and e == 1:
                    turn_output(0, ps_y[:].rearrange("p t d -> p (t d)"))
                if not last:
                    if e == AT_TURN_O:
                        turn_output(g + 1, ps_c[:].rearrange("p c t -> p (c t)"))
                    if e == AT_TURN_CW:
                        turn_routing(g + 1)

        turn_routing(0)
        pe.wait_ge(pick_2, 1)
        group(0, 0, first=True)
        with pe.Fori(0, PAIRS) as trip:
            for i in range(1, 3):
                group(trip * 2 + i, i % 2)
        group(NG - 1, 1, last=True)
        for e in range(NX - 2, NX):
            out_product(NG - 1, e)


_INS = ["L0_attn_x", "L0_attn_l_q1", "L0_attn_l_k1", "L0_attn_l_q2", "L0_attn_l_k2", "L0_attn_wqk",
        "L0_attn_wv", "L0_attn_wo", "L0_ffn_w_router", "L0_ffn_we1", "L0_ffn_we3", "L0_ffn_we2", "L0_ffn_ws1",
        "L0_ffn_ws3", "L0_ffn_ws2"]
_TURNED = {"L0_attn_wv", "L0_attn_wo"}


def kernel(**inputs):
    import numpy as _np
    import concourse.bacc as _bacc
    from concourse import mybir as _mybir
    from concourse.bass_utils import run_bass_kernel_spmd as _run

    nc = _bacc.Bacc("TRN2", target_bir_lowering=False, num_devices=1)
    arrays, args = {}, []
    wqk = _np.stack([_np.asarray(inputs["L0_attn_wq"]), _np.asarray(inputs["L0_attn_wk"])])
    wqk = wqk.reshape(2, 2, NH, DH, D).transpose(2, 4, 0, 1, 3).reshape(NH, D, 4 * DH)
    for name in _INS:
        a = wqk if name == "L0_attn_wqk" else _np.asarray(inputs[name])
        a = _np.ascontiguousarray(a.T if name in _TURNED else a)
        arrays[f"in_{name}"] = a
        args.append(nc.dram_tensor(f"in_{name}", a.shape, _mybir.dt.from_np(a.dtype), kind="ExternalInput").ap())
    out = nc.dram_tensor("out_0", (B, S, D), _mybir.dt.float32, kind="ExternalOutput").ap()
    o_dram = nc.dram_tensor("attention_out", (T, D), _mybir.dt.float32, kind="Internal").ap()
    xT_dram = nc.dram_tensor("tokens_turned", (NG, P, 2, DC, GRP), _mybir.dt.float32, kind="Internal").ap()
    build(nc, *args, out, o_dram, xT_dram)
    r = _run(nc, [arrays], core_ids=[0])
    return r.results[0]["out_0"]
```

```python
from contextlib import ExitStack
import math

import concourse.bass as bass
from concourse import mybir

F32 = mybir.dt.float32
F32R = mybir.dt.float32r
BF16 = mybir.dt.bfloat16
ALU = mybir.AluOpType
ACT = mybir.ActivationFunctionType
AX_X = mybir.AxisListType.X

P = 128
B, S, D = 4, 1024, 256
T = B * S
DC = D // P
NH = 8
DH = D // NH
NPAIR = B * NH
QB = S // P
GRP = 512
NG = T // GRP
GT = GRP // P
E, TOP_K, H, HS = 16, 4, 128, 512
NX = E + HS // H
WCOL = 2 * DC * H + D
WB = 4
NORM_G = DH // NH
L_INIT = 0.8 - 0.6 * math.exp(-0.3 * 1)
RMS_EPS = 1e-6
LN_EPS = 1e-5
SCALE = 1.0 / math.sqrt(DH)
MASKED = -1e30
NP = 4
STK = 3 * DH
NSTEP = 2 * QB
PARTS = [(h, i, k, min(k + GRP, (i + 1) * P)) for h in range(2) for i in range(QB)
         for k in range(0, (i + 1) * P, GRP)]
NPART = len(PARTS)
SIDE = {0: (0, 1, 0, 0), 1: (1, 1, 2, 1), 2: (1, 1, 1, 1), 3: (1, 1, 1, 1), 4: (1, 1, 2, 2), 5: (1, 1, 0, 1),
        6: (1, 0, 0, 0)}
WIDE_FROM = sum(sum(SIDE.get(c, ())) for c in range(QB // 2))
WIDE_TO = WIDE_FROM + 8
BANK = [(m - WIDE_FROM) % 4 if WIDE_FROM <= m < WIDE_TO else m % 2 for m in range(NPART)]
PROJECT_AT = 6
NB = 3


def wait(eng, sem, count):
    if not isinstance(count, int) or count > 0:
        eng.wait_ge(sem, count)


def build(nc, x, lq1, lk1, lq2, lk2, wqk, wvT, woT, wr, we1, we3, we2, ws1, ws3, ws2, out, o_dram, xT_dram):
    with ExitStack() as whole:
        keep = lambda n, s, d=F32: whole.enter_context(nc.sbuf_tensor(n, s, d))
        sem = lambda n: whole.enter_context(nc.semaphore(n))

        NW = NX * WCOL + DC * D
        with nc.sbuf_tensor("w_raw_all", [P, NW], F32) as w_raw_all:
            pass
        with nc.sbuf_tensor("w_lo_all", [P, NW], F32R) as w_lo_all:
            pass
        xT = keep("xT", [P, 2, DC, T], F32R)
        blocks = lambda a: (a[:, 0:NX * WCOL].rearrange("p (e n) -> p e n", n=WCOL),
                            a[:, NX * WCOL:NW].rearrange("p (c n) -> p c n", n=D))
        (w_raw, wo_raw), (w_lo, wo_lo) = blocks(w_raw_all), blocks(w_lo_all)
        raw_loaded = [sem(f"raw_loaded{i}") for i in range(NX // WB)]
        wo_loaded, xg_loaded = sem("wo_loaded"), sem("xg_loaded")
        o_free = [sem(f"o_free{i}") for i in range(NB)]
        cw_hl = keep("cw_hl", [P, T // P, 2 * E])
        ident = keep("ident", [P, P])
        lam_sum = keep("lam_sum", [P, 2])
        rms_eps = keep("rms_eps", [P, 1])
        x_tiles = x.rearrange("b (g t p) d -> (b g) p t d", p=P, t=GT)
        out_tiles = out.rearrange("b (g t p) d -> (b g) p t d", p=P, t=GT)

        with nc.sbuf_tensor("xg", [P, 2, 2, DC, GRP], F32R) as xg:
            pass
        with ExitStack() as early:
            v_all = early.enter_context(nc.sbuf_tensor("v_all", [P, T // P, D], F32))
            scores_r = early.enter_context(nc.sbuf_tensor("scores_r", [P, T // P, E], F32))
            wq_raw = early.enter_context(nc.sbuf_tensor("wq_raw", [P, DC, P], F32))
            wq_hi = early.enter_context(nc.sbuf_tensor("wq_hi", [P, DC, P], F32R))
            wq_lo = early.enter_context(nc.sbuf_tensor("wq_lo", [P, DC, P], F32R))
            pair_weights = (wq_raw, wq_hi, wq_lo, sem("w_loaded"), sem("w_rounded"), sem("w_split"))
            with ExitStack() as ctx:
                project_tokens(nc, ctx, x_tiles, (lq1, lk1, lq2, lk2), wvT, wr, xT, v_all, scores_r, ident,
                               lam_sum, rms_eps, wqk, pair_weights)
            with ExitStack() as ctx:
                attention(nc, ctx, wqk, pair_weights, xT, xT_dram, v_all, scores_r, cw_hl, ident, lam_sum, o_dram,
                          (woT, we1, we3, we2, ws1, ws3, ws2), w_raw, wo_raw, raw_loaded, wo_loaded, xg, xg_loaded,
                          o_free)
        with ExitStack() as ctx:
            feed_forward(nc, ctx, x_tiles, out_tiles, o_dram, xT_dram, w_raw, wo_raw, w_lo, wo_lo, raw_loaded,
                         wo_loaded, xg, xg_loaded, o_free, cw_hl, ident, rms_eps)


def project_tokens(nc, ctx, x_tiles, lams, wvT, wr, xT, v_all, scores_r, ident, lam_sum, rms_eps, wqk,
                   pair_weights):
    sb = lambda n, s, d=F32: ctx.enter_context(nc.sbuf_tensor(n, s, d))
    sem = lambda n: ctx.enter_context(nc.semaphore(n))
    NV = D + E
    x_in = sb("x_in", [P, 2, GT, D])
    xn = sb("xn", [P, 2, GT, D])
    stats = sb("stats", [P, 2, GT, 6])
    mean_var = sb("mean_var", [P, 2, GT, 2])
    std = sb("std", [P, 2, GT])
    rstd = sb("rstd", [P, 2, GT])
    turned = sb("turned", [P, 2, 2, DC, GRP], F32R)
    wv_raw = sb("wv_raw", [P, DC, NV])
    wv_hi = sb("wv_hi", [P, DC, NV], F32R)
    wv_lo = sb("wv_lo", [P, DC, NV], F32R)
    lam_in = sb("lam_in", [P, 4, NH])
    lam_prod = sb("lam_prod", [P, 2, NH])
    ln_eps = sb("ln_eps", [P, 1])
    ps_t = [ctx.enter_context(nc.psum_tensor(f"ps_t{i}", [P, DC, GRP], F32)) for i in range(2)]
    ps_v = ctx.enter_context(nc.psum_tensor("ps_v", [P, GT, 512], F32))

    x_loaded = [sem(f"x_loaded{i}") for i in range(2)]
    wv_loaded, lam_loaded = sem("wv_loaded"), sem("lam_loaded")
    zeroed, consts, ident_made = sem("zeroed"), sem("consts"), sem("ident_made")
    wv_rounded, wv_split = sem("wv_rounded"), sem("wv_split")
    bn_seen = sem("bn_seen")
    bn_done, stats_done, std_done, rstd_done, xn_done = (sem(n) for n in (
        "bn_done", "stats_done", "std_done", "rstd_done", "xn_done"))
    xt_in_psum, hi_done, lo_done, v_in_psum, v_copied, r_copied = (sem(n) for n in (
        "xt_in_psum", "hi_done", "lo_done", "v_in_psum", "v_copied", "r_copied"))
    kept = [sem(f"kept{i}") for i in range(2)]
    lam_a, lam_b = sem("lam_a"), sem("lam_b")

    w_raw, w_hi, w_lo, w_loaded, w_rounded, w_split = pair_weights

    block = ctx.enter_context(nc.Block())

    TRIPS = (NG - 4) // 2

    @block.sync
    def _(sp):
        def group(g, p, loads=True):
            if loads:
                sp.wait_ge(xn_done, g + 1)
                sp.dma_start(x_in[:, p], x_tiles[bass.ds(g + 2, 1)].rearrange("g p t d -> (g p) t d")
                             ).then_inc(x_loaded[p], 16)
            sp.wait_ge(lo_done, g + 1)
            sp.dma_start(xT[:, :, :, bass.ds(g * GRP, GRP)].bitcast(F32), turned[:, p].bitcast(F32)
                         ).then_inc(kept[p], 16)

        for g in range(2):
            sp.dma_start(x_in[:, g], x_tiles[g]).then_inc(x_loaded[g], 16)
        sp.dma_start(wv_raw[:, :, 0:D], wvT.rearrange("(c p) n -> p c n", p=P)).then_inc(wv_loaded, 16)
        sp.dma_start(wv_raw[:, :, D:NV], wr.rearrange("(c p) n -> p c n", p=P)).then_inc(wv_loaded, 16)
        for i, lam in enumerate(lams):
            sp.dma_start(lam_in[:, i, :], lam.partition_broadcast(P)).then_inc(lam_loaded, 16)
        sp.dma_start(w_raw[:], wqk[0].rearrange("(c p) m -> p c m", p=P)).then_inc(w_loaded, 16)
        group(0, 0)
        group(1, 1)
        with sp.Fori(1, TRIPS + 1) as trip:
            for p in range(2):
                group(trip * 2 + p, p)
        group(NG - 2, 0, loads=False)
        group(NG - 1, 1, loads=False)
        for p in range(2):
            sp.wait_ge(kept[p], 16 * (NG // 2))

    @block.gpsimd
    def _(pool):
        pool.memset(ident[:], 0.0).then_inc(zeroed, 1)
        pool.wait_ge(zeroed, 1)
        pool.affine_select(out=ident[:], in_=ident[:], compare_op=ALU.not_equal, fill=1.0, base=0,
                           pattern=[[-1, P]], channel_multiplier=1).then_inc(ident_made, 1)

    @block.vector
    def _(dve):
        def token_stats(g, p):
            dve.wait_ge(x_loaded[p], 16 * (g // 2 + 1))
            for t in range(GT):
                last = nc.vector.bn_stats(stats[:, p, t, :], x_in[:, p, t, :])
            last.then_inc(bn_done, 1)
            dve.wait_ge(bn_done, g + 1)
            dve.sem_inc(bn_seen, 1)
            for t in range(GT):
                last = nc.vector.bn_aggr(mean_var[:, p, t, :], stats[:, p, t, :])
            last.then_inc(stats_done, 1)

        def normalise(g, p):
            dve.wait_ge(std_done, g + 1)
            nc.vector.reciprocal(rstd[:, p], std[:, p]).then_inc(rstd_done, 1)
            dve.wait_ge(rstd_done, g + 1)
            if not (isinstance(g, int) and g < 2):
                dve.wait_ge(xt_in_psum, g - 1)
            for t in range(GT):
                last = nc.vector.tensor_scalar(xn[:, p, t, :], x_in[:, p, t, :], mean_var[:, p, t, 0:1],
                                               rstd[:, p, t:t + 1], ALU.subtract, ALU.mult)
            last.then_inc(xn_done, 1)

        def low_part(g, p):
            dve.wait_ge(hi_done, g + 1)
            nc.vector.tensor_tensor(turned[:, p, 1], ps_t[p][:], turned[:, p, 0].bitcast(F32), ALU.subtract
                                    ).then_inc(lo_done, 1)

        def router_out(g):
            dve.wait_ge(v_copied, g + 1)
            nc.vector.tensor_copy(scores_r[:, bass.ds(g * GT, GT), :], ps_v[:, :, D:NV]).then_inc(r_copied, 1)

        def group(g, p, normalises=True):
            if normalises:
                token_stats(g + 1, 1 - p)
            if not isinstance(g, int) or g >= 2:
                router_out(g - 2)
            low_part(g, p)
            if normalises:
                normalise(g + 1, 1 - p)

        nc.vector.memset(ln_eps[:], LN_EPS).then_inc(consts, 1)
        nc.vector.memset(rms_eps[:], RMS_EPS).then_inc(consts, 1)
        token_stats(0, 0)
        normalise(0, 0)
        group(0, 0)
        dve.wait_ge(wv_rounded, 1)
        nc.vector.tensor_tensor(wv_lo[:], wv_raw[:], wv_hi[:].bitcast(F32), ALU.subtract).then_inc(wv_split, 1)
        dve.wait_ge(w_rounded, 1)
        nc.vector.tensor_tensor(w_lo[:], w_raw[:], w_hi[:].bitcast(F32), ALU.subtract).then_inc(w_split, 1)
        dve.wait_ge(lam_loaded, 64)
        nc.vector.tensor_tensor(lam_prod[:], lam_in[:, 0::2, :], lam_in[:, 1::2, :], ALU.mult).then_inc(lam_a, 1)
        dve.wait_ge(lam_a, 1)
        nc.vector.tensor_reduce(lam_sum[:], lam_prod[:], AX_X, ALU.add).then_inc(lam_b, 1)
        group(1, 1)
        with dve.Fori(1, TRIPS + 1) as trip:
            for p in range(2):
                group(trip * 2 + p, p)
        group(NG - 2, 0)
        group(NG - 1, 1, normalises=False)
        router_out(NG - 2)
        router_out(NG - 1)

    @block.scalar
    def _(act):
        def root(g, p):
            act.wait_ge(stats_done, g + 1)
            nc.scalar.activation(std[:, p], mean_var[:, p, :, 1], ACT.Sqrt, bias=ln_eps[:]).then_inc(std_done, 1)

        def high_part(g, p):
            act.wait_ge(xt_in_psum, g + 1)
            if not isinstance(g, int) or g >= 2:
                act.wait_ge(kept[p], 16 * (g // 2))
            nc.scalar.activation(turned[:, p, 0], ps_t[p][:], ACT.Copy).then_inc(hi_done, 1)

        def values_out(g):
            act.wait_ge(v_in_psum, g + 1)
            nc.scalar.activation(v_all[:, bass.ds(g * GT, GT), :], ps_v[:, :, 0:D], ACT.Copy).then_inc(v_copied, 1)

        def group(g, p, normalises=True):
            high_part(g, p)
            if normalises:
                root(g + 1, 1 - p)
            if not isinstance(g, int) or g >= 1:
                values_out(g - 1)

        act.wait_ge(consts, 2)
        root(0, 0)
        group(0, 0)
        act.wait_ge(wv_loaded, 32)
        nc.scalar.activation(wv_hi[:], wv_raw[:], ACT.Copy).then_inc(wv_rounded, 1)
        act.wait_ge(w_loaded, 16)
        nc.scalar.activation(w_hi[:], w_raw[:], ACT.Copy).then_inc(w_rounded, 1)
        group(1, 1)
        with act.Fori(1, TRIPS + 1) as trip:
            for p in range(2):
                group(trip * 2 + p, p)
        group(NG - 2, 0)
        group(NG - 1, 1, normalises=False)
        values_out(NG - 1)

    @block.tensor
    def _(pe):
        pe.wait_ge(ident_made, 1)

        def transposes(g, p):
            pe.wait_ge(xn_done, g + 1)
            for c in range(DC):
                for t in range(GT):
                    last = nc.tensor.transpose(ps_t[p][:, c, t * P:(t + 1) * P], xn[:, p, t, c * P:(c + 1) * P],
                                               ident[:])
            last.then_inc(xt_in_psum, 1)

        def values(g, p):
            if isinstance(g, int) and g == 0:
                pe.wait_ge(wv_split, 1)
            else:
                pe.wait_ge(r_copied, g)
            pe.wait_ge(lo_done, g + 1)
            for t in range(GT):
                cols = slice(t * P, (t + 1) * P)
                n = 0
                for c in range(DC):
                    for a, b in ((0, wv_hi), (0, wv_lo), (1, wv_hi)):
                        n += 1
                        last = nc.tensor.matmul(ps_v[:, t, 0:NV], turned[:, p, a, c, cols], b[:, c, :],
                                                start=(n == 1), stop=(n == 3 * DC))
            last.then_inc(v_in_psum, 1)

        def group(g, p):
            transposes(g, p)
            if not isinstance(g, int) or g >= 1:
                values(g - 1, 1 - p)

        group(0, 0)
        group(1, 1)
        with pe.Fori(1, TRIPS + 1) as trip:
            for p in range(2):
                group(trip * 2 + p, p)
        group(NG - 2, 0)
        group(NG - 1, 1)
        values(NG - 1, 1)


def attention(nc, ctx, wqk, pair_weights, xT, xT_dram, v_all, scores_r, cw_hl, ident, lam_sum, o_dram,
              late_weights, w_late, wo_late, raw_loaded, wo_loaded, xg, xg_loaded, o_free):
    sb = lambda n, s, d=F32: ctx.enter_context(nc.sbuf_tensor(n, s, d))
    sem = lambda n: ctx.enter_context(nc.semaphore(n))
    xT_hi, xT_lo = xT[:, 0], xT[:, 1]
    w_raw, w_hi, w_lo, w_loaded, w_rounded, w_split = pair_weights
    qk_hi = sb("qk_hi", [P, S], F32R)
    qk_lo = sb("qk_lo", [P, S], F32R)
    stack = sb("stack", [P, NB, 4, S], F32R)
    v_ones = sb("v_ones", [P, NB, QB, 2 * DH])
    probs = sb("probs", [P, NP, S])
    part_max = sb("part_max", [P, NB, 2 * QB, 2])
    row_max = sb("row_max", [P, NB, 2 * QB])
    max_row = sb("max_row", [2 * QB, P], F32R)
    o_raw = sb("o_raw", [P, S])
    rden = sb("rden", [P, QB, 2])
    rlam = sb("rlam", [P, QB])
    o_a = sb("o_a", [P, QB, DH])
    o_b = sb("o_b", [P, QB, DH])
    o_pair = sb("o_pair", [P, NB, QB, DH])
    mask = sb("mask", [P, GRP])
    masked_part = sb("masked_part", [P, 4, GRP], BF16)
    lam_exp = sb("lam_exp", [P, 2])
    neg_lam = sb("neg_lam", [P, 1])
    top = sb("top", [P, T // P])
    gate = sb("gate", [P, T // P, E])
    rank = sb("rank", [P, T // P, E])
    beats = sb("beats", [P, T // P, E])
    gate_sum = sb("gate_sum", [P, T // P])
    gate_inv = sb("gate_inv", [P, T // P])
    ps_s = [ctx.enter_context(nc.psum_tensor(f"ps_s{i}", [P, S], F32)) for i in range(2)]
    ps_x = ctx.enter_context(nc.psum_tensor("ps_x", [P, S], F32))
    ps_o = ctx.enter_context(nc.psum_tensor("ps_o", [P, S], F32))

    mask_0, mask_1, ones_a, ones_b = (sem(n) for n in ("mask_0", "mask_1", "ones_a", "ones_b"))
    projected, hi_out, lo_out, stacked = (sem(n) for n in ("projected", "hi_out", "lo_out", "stacked"))
    side_scores, side_max, max_joined, max_filled, max_in_psum, max_turned, max_placed = (sem(n) for n in (
        "side_scores", "side_max", "max_joined", "max_filled", "max_in_psum", "max_turned", "max_placed"))
    scored, exped, cut, pv_done, v_staged = (sem(n) for n in ("scored", "exped", "cut", "pv_done", "v_staged"))
    o_copied, o_turned, rden_done, rlam_done, oa_done, ob_done, o_done = (sem(n) for n in (
        "o_copied", "o_turned", "rden_done", "rlam_done", "oa_done", "ob_done", "o_done"))
    ranked, v_filled, tokens_saved = sem("ranked"), sem("v_filled"), sem("tokens_saved")
    lam_a, lam_b, top_done, shift_done, gate_done = (sem(n) for n in (
        "lam_c", "lam_d", "top_done", "shift_done", "gate_done"))
    part_seen, exp_seen = sem("part_seen"), sem("exp_seen")

    Q, K = (0, 1), (2, 3)
    o_view = o_dram.rearrange("(b i p) d -> b p i d", p=P, i=QB)

    def projection(n, half):
        if isinstance(n, int) and n < NB:
            return (ps_x, ps_s[0], ps_s[1])[n][:, half * GRP:(half + 1) * GRP]
        return ps_s[half][:, 0:GRP]

    def bank_of(n, m):
        return m % 4 if isinstance(n, int) and n == 0 else BANK[m]

    def part_bank(n, m):
        bank = bank_of(n, m)
        if bank >= 2 and isinstance(n, int) and n == 0:
            return ps_o[:, (bank - 2) * GRP:(bank - 1) * GRP]
        return ps_x[:, bank * GRP:(bank + 1) * GRP] if bank < 2 else ps_s[bank - 2][:, 0:GRP]

    def had_bank(n, m):
        return max((k for k in range(m) if bank_of(n, k) == bank_of(n, m)), default=-1)

    block = ctx.enter_context(nc.Block())
    TRIPS = (NPAIR - 5) // NB

    @block.sync
    def _(sp):
        def load_weights(n):
            src = wqk[bass.ds(n % NH, 1)].rearrange("j (c p) m -> (j p) c m", p=P)
            wait(sp, w_split, n)
            sp.dma_start(w_raw[:], src).then_inc(w_loaded, 16)

        def stack_pair(n, p):
            sp.wait_ge(lo_out, 2 * (n + 1))
            for h in range(2):
                q, k = h * DH, (2 + h) * DH
                for src, row, place, at in ((qk_hi, q, Q[h], 0), (qk_lo, q, Q[h], DH), (qk_hi, q, Q[h], 2 * DH),
                                            (qk_hi, k, K[h], 0), (qk_hi, k, K[h], DH), (qk_lo, k, K[h], 2 * DH)):
                    sp.dma_start(stack[at:at + DH, p, place, :].bitcast(F32),
                                 src[row:row + DH, :].bitcast(F32)).then_inc(stacked, 16)

        def place_max(n, p):
            sp.wait_ge(max_turned, n + 1)
            sp.dma_start(stack[STK:STK + 1, p, 0:2, :].rearrange("r h s -> r (h s)").bitcast(F32),
                         max_row[:].bitcast(F32)).then_inc(max_placed, 16)

        def store(n, p):
            dst = o_view[bass.ds(n // NH, 1), :, :, bass.ds((n % NH) * DH, DH)].rearrange("b p i d -> (b p) i d")
            sp.wait_ge(o_done, n + 1)
            sp.dma_start(dst, o_pair[:, p]).then_inc(o_free[p], 16)

        def save_tokens(t):
            dst = xT_dram[bass.ds(t // GT, 1), :, :, :, bass.ds((t % GT) * P, P)]
            sp.dma_start(dst.rearrange("g p a c t -> (g p) a c t"),
                         xT[:, :, :, bass.ds(t * P, P)].bitcast(F32)).then_inc(tokens_saved, 16)

        def load_late(b):
            woT, we1, we3, we2, ws1, ws3, ws2 = late_weights
            dst = w_late[:, b * WB:(b + 1) * WB, :]
            for i, (w, ws) in enumerate(((we1, ws1), (we3, ws3))):
                for c in range(DC):
                    rows = slice(c * P, (c + 1) * P)
                    src = (w[b * WB:(b + 1) * WB, rows, :].rearrange("e p h -> p e h") if b * WB < E
                           else ws[rows, :].rearrange("p (e h) -> p e h", h=H))
                    at = (i * DC + c) * H
                    sp.dma_start(dst[:, :, at:at + H], src).then_inc(raw_loaded[b], 16)
            src = (we2[b * WB:(b + 1) * WB].rearrange("e h d -> h e d") if b * WB < E
                   else ws2.rearrange("(e h) d -> h e d", h=H))
            sp.dma_start(dst[:, :, 2 * DC * H:WCOL], src).then_inc(raw_loaded[b], 16)

        def step(n, p, stack_next=True, place=True, weights=True, stores=True, saves=True):
            if stack_next:
                stack_pair(n + 2, (p + 2) % NB)
            if saves:
                save_tokens(n + NB)
            if stores:
                store(n - 1, (p - 1) % NB)
            if weights:
                load_weights(n + 4)
            if place:
                place_max(n + 1, (p + 1) % NB)

        load_weights(1)
        load_weights(2)
        stack_pair(0, 0)
        stack_pair(1, 1)
        load_weights(3)
        place_max(0, 0)
        for t in range(NB):
            save_tokens(t)
        step(0, 0, stores=False)
        with sp.Fori(0, TRIPS) as trip:
            for i in range(NB):
                step(trip * NB + (1 + i), (1 + i) % NB)
        n = TRIPS * NB + 1
        step(n, n % NB, weights=False)
        step(n + 1, (n + 1) % NB, weights=False, saves=False)
        sp.wait_ge(tokens_saved, 16 * (T // P))
        load_late(0)
        load_late(1)
        step(n + 2, (n + 2) % NB, stack_next=False, weights=False, saves=False)
        load_late(2)
        sp.dma_start(wo_late, late_weights[0].rearrange("(c p) n -> p c n", p=P)).then_inc(wo_loaded, 16)
        load_late(3)
        load_late(4)
        step(n + 3, (n + 3) % NB, stack_next=False, weights=False, place=False, saves=False)
        sp.wait_ge(v_staged, NPAIR)
        sp.dma_start(xg[:, 0].bitcast(F32), xT_dram[0]).then_inc(xg_loaded, 16)
        store(NPAIR - 1, (NPAIR - 1) % NB)

    @block.gpsimd
    def _(pool):
        pool.memset(mask[:], 0.0).then_inc(mask_0, 1)
        pool.wait_ge(mask_0, 1)
        pool.affine_select(out=mask[:, GRP - P:GRP], in_=mask[:, GRP - P:GRP], compare_op=ALU.is_ge, fill=MASKED,
                           base=0, pattern=[[-1, P]], channel_multiplier=1).then_inc(mask_1, 1)
        pool.memset(v_ones[:], 1.0).then_inc(v_filled, 1)
        pool.wait_ge(v_filled, 1)

        for p in range(NB):
            pool.memset(o_pair[:, p], 0.0).then_inc(o_free[p], 16)

        def stage_values(n, p):
            if not isinstance(n, int) or n >= NB:
                pool.wait_ge(pv_done, QB * (n - NB + 1))
            pool.tensor_copy(v_ones[:, p, :, 0:DH],
                             v_all[:, bass.ds((n // NH) * QB, QB), bass.ds((n % NH) * DH, DH)]).then_inc(v_staged, 1)

        def cut_diagonal(n, c, h):
            at = (2 * c + h) % NP
            pool.wait_ge(exped, NSTEP * n + 2 * c + h + 1)
            pool.sem_inc(exp_seen, 1)
            pool.affine_select(out=probs[:, at, c * P:(c + 1) * P], in_=probs[:, at, c * P:(c + 1) * P],
                               compare_op=ALU.is_ge, fill=0.0, base=0, pattern=[[1, P]], channel_multiplier=-1
                               ).then_inc(cut, 1)

        def split_weights(n):
            pool.wait_ge(w_rounded, n + 1)
            pool.tensor_tensor(w_lo[:], w_raw[:], w_hi[:].bitcast(F32), ALU.subtract).then_inc(w_split, 1)

        def add_heads(n, p):
            pool.wait_ge(ob_done, n + 1)
            pool.wait_ge(o_free[p], (n // NB) * 16 + 16)
            pool.tensor_tensor(o_pair[:, p], o_a[:], o_b[:], ALU.add).then_inc(o_done, 1)

        def step(n, p, adds=True, splits=True, stages=True):
            for c in range(QB):
                for h in range(2):
                    cut_diagonal(n, c, h)
                if c == 1 and adds:
                    add_heads(n - 1, (p - 1) % NB)
                if c == 2 and splits:
                    split_weights(n + 3)
                if c == 4 and stages:
                    stage_values(n + 2, (p + 2) % NB)

        split_weights(1)
        split_weights(2)
        for n in range(2):
            stage_values(n, n)
        step(0, 0, adds=False)
        with pool.Fori(0, TRIPS) as trip:
            for i in range(NB):
                step(trip * NB + (1 + i), (1 + i) % NB)
        for n in range(TRIPS * NB + 1, NPAIR):
            step(n, n % NB, splits=n + 3 < NPAIR, stages=n + 2 < NPAIR)
        add_heads(NPAIR - 1, (NPAIR - 1) % NB)

    @block.tensor
    def _(pe):
        def project(n, half, chunks=range(DC)):
            pe.wait_ge(w_split, n + 1)
            if chunks[0] == 0 and (not isinstance(n, int) or n >= NB):
                last_part = max(m for m in range(NPART) if BANK[m] == 2 + half)
                pe.wait_ge(side_max, NPART * (n - 2) + last_part + 1)
            for c in chunks:
                for i, (w, xt) in enumerate(((w_hi, xT_hi), (w_lo, xT_hi), (w_hi, xT_lo))):
                    last = nc.tensor.matmul(projection(n, half), w[:, c, :],
                                            xt[:, c, bass.ds((n // NH) * S + half * GRP, GRP)],
                                            start=(c == 0 and i == 0), stop=(c == DC - 1 and i == 2))
            if chunks[-1] == DC - 1:
                last.then_inc(projected, 1)

        def side(n, p, m):
            h, i, k0, k1 = PARTS[m]
            if m == 0:
                pe.wait_ge(stacked, 192 * (n + 1))
                if isinstance(n, int) and n == 1:
                    pe.wait_ge(max_turned, 1)
                elif not isinstance(n, int) or n > 1:
                    pe.wait_ge(ob_done, n - 1)
            before = had_bank(n, m)
            if before >= 0:
                pe.wait_ge(side_max, NPART * n + before + 1)
            last = nc.tensor.matmul(part_bank(n, m)[:, 0:k1 - k0], stack[0:STK, p, Q[h], i * P:(i + 1) * P],
                                    stack[0:STK, p, K[h], k0:k1], start=True, stop=True)
            last.then_inc(side_scores, 1)

        def turn_max(n, p):
            pe.wait_ge(max_joined, n + 1)
            nc.tensor.transpose(ps_x[0:2 * QB, GRP:GRP + P], row_max[:, p, :], ident[:]).then_inc(max_in_psum, 1)

        def score(n, p, c, h):
            s = 2 * c + h
            if s == 0:
                pe.wait_ge(max_placed, 16 * (n + 1))
            if s < 2 and isinstance(n, int) and n == 0:
                pe.wait_ge(lo_out, 2 * (s + 2))
            elif s < 2 and not (isinstance(n, int) and n + 2 >= NPAIR):
                pe.wait_ge(lo_out, 2 * (n + 2) + s + 1)
            if not (isinstance(n, int) and n == 0 and s < 2):
                pe.wait_ge(exped, NSTEP * n + s - 1)
            ps = ps_s[h]
            q0 = c * P
            while q0 < S:
                q1 = min((q0 // GRP + 1) * GRP, S)
                last = nc.tensor.matmul(ps[:, q0:q1], stack[0:STK + 1, p, K[h], c * P:(c + 1) * P],
                                        stack[0:STK + 1, p, Q[h], q0:q1], start=True, stop=True)
                q0 = q1
            last.then_inc(scored, 1)

        def value(n, p, c, bank):
            q0, q1 = max(c * P, bank * GRP), (bank + 1) * GRP
            if c == 0 and bank == 0:
                pe.wait_ge(v_staged, n + 1)
                wait(pe, o_copied, n)
            if q1 <= q0:
                return
            if q0 == c * P:
                pe.wait_ge(cut, NSTEP * n + 2 * c + 2)
            for h in range(2):
                last = nc.tensor.matmul(ps_o[h * 64:(h + 1) * 64, q0:q1], v_ones[:, p, c, :],
                                        probs[:, (2 * c + h) % NP, q0:q1], start=(c == 0),
                                        stop=(c * P + P >= q1))
            if bank == 1:
                last.then_inc(pv_done, 1)

        def turn_out(n):
            pe.wait_ge(o_copied, n + 1)
            if isinstance(n, int) and n == NPAIR - 1:
                pe.wait_ge(ob_done, n)
            else:
                pe.wait_ge(max_turned, n + 2)
            for i in range(QB):
                last = nc.tensor.transpose(ps_x[:, i * P:(i + 1) * P], o_raw[:, i * P:(i + 1) * P], ident[:])
            last.then_inc(o_turned, 1)

        def step(n, p, sides=True, projects=True):
            parts = iter(range(NPART) if sides else ())

            def some(count):
                for _, m in zip(range(count), parts):
                    side(n + 1, (p + 1) % NB, m)

            for c in range(QB):
                after = SIDE.get(c, (0, 0, 0, 0))
                for h in range(2):
                    score(n, p, c, h)
                    some(after[h])
                if c == PROJECT_AT and projects:
                    project(n + 3, 0, range(0, DC // 2))
                if c > 0:
                    for bank in range(2):
                        value(n, p, c - 1, bank)
                        some(after[2 + bank])
            if sides:
                turn_max(n + 1, (p + 1) % NB)
            if projects:
                project(n + 3, 0, range(DC // 2, DC))
            value(n, p, QB - 1, 1)
            if projects:
                project(n + 3, 1)
            turn_out(n)

        for n in range(NB):
            project(n, 0)
            project(n, 1)
        pe.wait_ge(lo_out, 2)
        for m in range(NPART):
            side(0, 0, m)
        turn_max(0, 0)
        pe.wait_ge(ones_b, 1)
        step(0, 0)
        with pe.Fori(0, TRIPS) as trip:
            for i in range(NB):
                step(trip * NB + (1 + i), (1 + i) % NB)
        n = TRIPS * NB + 1
        step(n, n % NB)
        step(n + 1, (n + 1) % NB, projects=False)
        step(n + 2, (n + 2) % NB, projects=False)
        step(n + 3, (n + 3) % NB, sides=False, projects=False)

    @block.scalar
    def _(act):
        def round_weights(n):
            act.wait_ge(w_loaded, 16 * (n + 1))
            wait(act, projected, 2 * n)
            nc.scalar.activation(w_hi[:], w_raw[:], ACT.Copy).then_inc(w_rounded, 1)

        def high_part(n, half):
            cols = slice(half * GRP, (half + 1) * GRP)
            act.wait_ge(projected, 2 * n + half + 1)
            if half == 0:
                wait(act, stacked, 192 * n)
            nc.scalar.activation(qk_hi[:, cols], projection(n, half), ACT.Copy).then_inc(hi_out, 1)

        def exp(n, c, h):
            s = 2 * c + h
            act.wait_ge(scored, NSTEP * n + s + 1)
            if not (isinstance(n, int) and n == 0 and s < NP):
                act.wait_ge(pv_done, QB * n + c - NP // 2 + 1)
            nc.scalar.activation(probs[:, s % NP, c * P:S], ps_s[h][:, c * P:S], ACT.Exp, scale=SCALE
                                 ).then_inc(exped, 1)

        def step(n, projects=True):
            for c in range(QB):
                for h in range(2):
                    exp(n, c, h)
                if projects and c == 1:
                    round_weights(n + 3)
            if projects:
                high_part(n + 3, 0)
                high_part(n + 3, 1)

        nc.scalar.activation(lam_exp[:], lam_sum[:], ACT.Exp).then_inc(lam_a, 1)
        for n in range(NB):
            high_part(n, 0)
            high_part(n, 1)
            if n == 0:
                round_weights(1)
                round_weights(2)
                act.wait_ge(ones_a, 1)
                for p in range(NB):
                    for h in range(2):
                        last = nc.scalar.activation(stack[STK:STK + 1, p, K[h], :], o_raw[STK:STK + 1, :], ACT.Copy)
                last.then_inc(ones_b, 1)
        step(0)
        with act.Fori(0, TRIPS) as trip:
            for i in range(NB):
                step(trip * NB + 1 + i)
        n = TRIPS * NB + 1
        step(n)
        act.wait_ge(shift_done, 1)
        nc.scalar.activation(gate[:], gate[:], ACT.Exp).then_inc(gate_done, 1)
        for k in range(n + 1, NPAIR):
            step(k, projects=False)

    @block.vector
    def _(dve):
        def low_part(n, half):
            cols = slice(half * GRP, (half + 1) * GRP)
            dve.wait_ge(hi_out, 2 * n + half + 1)
            nc.vector.tensor_tensor(qk_lo[:, cols], projection(n, half), qk_hi[:, cols].bitcast(F32), ALU.subtract
                                    ).then_inc(lo_out, 1)

        def side_maxima(n, p, m):
            h, i, k0, k1 = PARTS[m]
            dve.wait_ge(side_scores, NPART * n + m + 1)
            if k1 == (i + 1) * P:
                dve.sem_inc(part_seen, 1)
            width = k1 - k0
            out, part = part_max[:, p, h * QB + i, k0 // GRP:k0 // GRP + 1], part_bank(n, m)[:, 0:width]
            if k1 == (i + 1) * P:
                nc.vector.tensor_tensor_reduce(masked_part[:, m % 4, 0:width], part, mask[:, GRP - width:GRP], 1.0,
                                               -3e38, ALU.add, ALU.max, out).then_inc(side_max, 1)
            else:
                nc.vector.tensor_reduce(out, part, AX_X, ALU.max).then_inc(side_max, 1)

        def join_maxima(n, p):
            dve.wait_ge(side_max, NPART * (n + 1))
            nc.vector.tensor_reduce(row_max[:, p, :], part_max[:, p], AX_X, ALU.max).then_inc(max_joined, 1)

        def negate_max(n):
            dve.wait_ge(max_in_psum, n + 1)
            wait(dve, max_placed, 16 * n)
            nc.vector.tensor_scalar(max_row[:], ps_x[0:2 * QB, GRP:GRP + P], -1.0, None, ALU.mult
                                    ).then_inc(max_turned, 1)

        def copy_out(n):
            dve.wait_ge(pv_done, QB * (n + 1))
            wait(dve, o_turned, n)
            nc.vector.tensor_copy(o_raw[:], ps_o[:]).then_inc(o_copied, 1)

        def combine(n):
            turned = ps_x[:].rearrange("q (i f) -> q i f", f=P)
            dve.wait_ge(o_turned, n + 1)
            nc.vector.reciprocal(rden[:], turned[:, :, DH::2 * DH]).then_inc(rden_done, 1)
            dve.wait_ge(rden_done, n + 1)
            wait(dve, o_done, n)
            nc.vector.tensor_scalar(rlam[:], rden[:, :, 1], neg_lam[:, 0:1], None, ALU.mult).then_inc(rlam_done, 1)
            nc.vector.tensor_tensor(o_a[:], turned[:, :, 0:DH], rden[:, :, 0:1].broadcast_to([P, QB, DH]), ALU.mult
                                    ).then_inc(oa_done, 1)
            dve.wait_ge(rlam_done, n + 1)
            nc.vector.tensor_tensor(o_b[:], turned[:, :, 2 * DH:3 * DH],
                                    rlam[:].unsqueeze(2).broadcast_to([P, QB, DH]), ALU.mult).then_inc(ob_done, 1)

        def rank_by(f, add):
            dve.wait_ge(ranked, 2 * f + 1 + add)
            if add:
                nc.vector.tensor_tensor(rank[:], rank[:], beats[:], ALU.add).then_inc(ranked, 1)
                return
            for lo, hi, op in ((0, f + 1, ALU.is_gt), (f + 1, E, ALU.is_ge)):
                if hi > lo:
                    last = nc.vector.tensor_tensor(
                        beats[:, :, lo:hi], scores_r[:, :, f:f + 1].broadcast_to([P, T // P, hi - lo]),
                        scores_r[:, :, lo:hi], op)
            last.then_inc(ranked, 1)

        def routing_weights():
            dve.wait_ge(ranked, 2 * E + 1)
            dve.wait_ge(gate_done, 1)
            nc.vector.scalar_tensor_tensor(out=gate[:], in0=rank[:], scalar=TOP_K - 0.5, in1=gate[:], op0=ALU.is_lt,
                                           op1=ALU.mult).then_inc(ranked, 1)
            dve.wait_ge(ranked, 2 * E + 2)
            nc.vector.tensor_reduce(gate_sum[:], gate[:], AX_X, ALU.add).then_inc(ranked, 1)
            dve.wait_ge(ranked, 2 * E + 3)
            nc.vector.reciprocal(gate_inv[:], gate_sum[:]).then_inc(ranked, 1)
            dve.wait_ge(ranked, 2 * E + 4)
            nc.vector.scalar_tensor_tensor(out=gate[:], in0=gate[:], scalar=TOP_K / (TOP_K + 1.0),
                                           in1=gate_inv[:].unsqueeze(2).broadcast_to([P, T // P, E]),
                                           op0=ALU.mult, op1=ALU.mult).then_inc(ranked, 1)
            dve.wait_ge(ranked, 2 * E + 5)
            nc.vector.tensor_copy(cw_hl[:, :, 0:E].bitcast(F32R), gate[:]).then_inc(ranked, 1)
            dve.wait_ge(ranked, 2 * E + 6)
            nc.vector.tensor_tensor(cw_hl[:, :, E:2 * E], gate[:], cw_hl[:, :, 0:E], ALU.subtract).then_inc(ranked, 1)

        def step(n, p, sides=True, projects=True, turns=True, ranks=None):
            if turns:
                combine(n - 1)
            if sides:
                for m in range(NPART):
                    side_maxima(n + 1, (p + 1) % NB, m)
                    if ranks is not None and m % 2 == 0 and ranks + m // 2 < 2 * E:
                        rank_by((ranks + m // 2) // 2, (ranks + m // 2) % 2)
                join_maxima(n + 1, (p + 1) % NB)
                negate_max(n + 1)
            copy_out(n)
            if projects:
                low_part(n + 3, 0)
                low_part(n + 3, 1)

        nc.vector.memset(o_raw[STK:STK + 1, :], 1.0).then_inc(ones_a, 1)
        nc.vector.memset(part_max[:], -3e38).then_inc(max_filled, 1)
        dve.wait_ge(max_filled, 1)
        dve.wait_ge(mask_1, 1)
        low_part(0, 0)
        low_part(0, 1)
        low_part(1, 0)
        low_part(1, 1)
        for m in range(NPART):
            side_maxima(0, 0, m)
        join_maxima(0, 0)
        negate_max(0)
        low_part(2, 0)
        low_part(2, 1)
        dve.wait_ge(lam_a, 1)
        nc.vector.tensor_tensor(neg_lam[:], lam_exp[:, 1:2], lam_exp[:, 0:1], ALU.subtract).then_inc(lam_b, 1)
        dve.wait_ge(lam_b, 1)
        nc.vector.tensor_scalar(neg_lam[:], neg_lam[:], -L_INIT, None, ALU.add).then_inc(lam_b, 1)
        dve.wait_ge(lam_b, 2)
        step(0, 0, turns=False)
        with dve.Fori(0, TRIPS) as trip:
            for i in range(NB):
                step(trip * NB + (1 + i), (1 + i) % NB)
        n = TRIPS * NB + 1
        nc.vector.tensor_reduce(top[:], scores_r[:], AX_X, ALU.max).then_inc(top_done, 1)
        dve.wait_ge(top_done, 1)
        nc.vector.tensor_tensor(gate[:], scores_r[:], top[:].unsqueeze(2).broadcast_to([P, T // P, E]), ALU.subtract
                                ).then_inc(shift_done, 1)
        nc.vector.memset(rank[:], 0.0).then_inc(ranked, 1)
        step(n, n % NB, ranks=0)
        step(n + 1, (n + 1) % NB, projects=False, ranks=NPART // 2)
        step(n + 2, (n + 2) % NB, projects=False, ranks=NPART)
        routing_weights()
        step(n + 3, (n + 3) % NB, sides=False, projects=False)
        combine(NPAIR - 1)


def feed_forward(nc, ctx, x_tiles, out_tiles, o_dram, xT_dram, w_raw, wo_raw, w_lo, wo_lo, raw_loaded, wo_loaded,
                 xg, xg_loaded, o_free, cw_hl, ident, rms_eps):
    sb = lambda n, s, d=F32: ctx.enter_context(nc.sbuf_tensor(n, s, d))
    sem = lambda n: ctx.enter_context(nc.semaphore(n))
    sb("xg_place", [P, 2, 2, DC, GRP], F32R)
    w_hi = sb("we_hi", [P, NX, WCOL], F32R)
    wo_hi = sb("wo_hi", [P, DC, D], F32R)
    pick_f = sb("pick_f", [2 * E, E])
    pick = sb("pick", [2 * E, E], F32R)
    cw_st = sb("cw_st", [P, GT, 2 * E])
    cwT = sb("cwT", [2 * E, GRP], F32R)
    o_in = sb("o_in", [P, GT, D])
    ms = sb("ms", [P, GT, D // NORM_G])
    on = sb("on", [P, GT, D])
    oT_hi = sb("oT_hi", [P, DC, GRP], F32R)
    oT_lo = sb("oT_lo", [P, DC, GRP], F32R)
    res = sb("res", [P, GT, D])
    act_h = sb("act_h", [P, 2, GRP])
    mid = sb("mid", [P, 2, GRP])
    hid = sb("hid", [P, 2, GRP])
    hid_hi = sb("hid_hi", [P, 2, GRP], F32R)
    hid_lo = sb("hid_lo", [P, 2, GRP], F32R)
    ps_h = [ctx.enter_context(nc.psum_tensor(f"ps_h{i}", [P, 2, GRP], F32)) for i in range(2)]
    ps_c = ctx.enter_context(nc.psum_tensor("ps_c", [P, 2, GRP], F32))
    ps_y = ctx.enter_context(nc.psum_tensor("ps_y", [P, GT, D], F32))

    w_rounded, w_split, wo_rounded, wo_split = (sem(n) for n in ("we_rounded", "we_split", "wo_rounded", "wo_split"))
    pick_0, pick_1, pick_2 = (sem(n) for n in ("pick_0", "pick_1", "pick_2"))
    cw_staged, cw_turned, cwT_done = (sem(n) for n in ("cw_staged", "cw_turned", "cwT_done"))
    o_loaded, x_loaded, sq_done, ms_done, rms_done, rr_done, on_done, o_turned, oT_rounded, oT_split = (
        sem(n) for n in ("f_o_loaded", "f_x_loaded", "sq_done", "ms_done", "rms_done", "rr_done",
                         "on_done", "f_o_turned", "oT_rounded", "oT_split"))
    h_ready, c_ready, silu_done, mid_done, hid_done, hi_done, lo_done, y_part, res_done, stored = (sem(n) for n in (
        "h_ready", "c_ready", "silu_done", "mid_done", "hid_done", "f_hi_done", "f_lo_done", "y_part", "res_done",
        "stored"))
    o_tiles = o_dram.rearrange("(g t p) d -> g p t d", p=P, t=GT)
    one = lambda ap: ap.rearrange("g p t d -> (g p) t d")
    AT_SQUARE, AT_SUM, AT_ROOT, AT_SCALE, AT_TURN_O, AT_TURN_CW = 6, 7, 8, 9, E + 1, E + 3
    PAIRS = (NG - 2) // 2

    block = ctx.enter_context(nc.Block())

    @block.sync
    def _(sp):
        def load_tokens(g, p):
            sp.dma_start(xg[:, p].bitcast(F32), xT_dram[bass.ds(g, 1)].rearrange("g p a c t -> (g p) a c t")
                         ).then_inc(xg_loaded, 16)

        def group(g, p, last=False):
            if not last:
                sp.wait_ge(h_ready, g * NX + 1)
                load_tokens(g + 1, 1 - p)
                sp.wait_ge(on_done, g + 1)
                sp.dma_start(o_in[:], one(o_tiles[bass.ds(g + 1, 1)])).then_inc(o_loaded, 16)
            sp.wait_ge(res_done, g + 1)
            sp.dma_start(one(out_tiles[bass.ds(g, 1)]), res[:]).then_inc(stored, 16)
            if not last:
                sp.wait_ge(stored, 16 * (g + 1))
                sp.dma_start(res[:], one(x_tiles[bass.ds(g + 1, 1)])).then_inc(x_loaded, 16)

        for p in range(NB):
            sp.wait_ge(o_free[p], 16 * (1 + (NPAIR - 1 - p) // NB + 1))
        sp.dma_start(o_in[:], o_tiles[0]).then_inc(o_loaded, 16)
        sp.dma_start(res[:], x_tiles[0]).then_inc(x_loaded, 16)
        group(0, 0)
        with sp.Fori(0, PAIRS) as trip:
            for i in range(1, 3):
                group(trip * 2 + i, i % 2)
        group(NG - 1, 1, last=True)
        sp.wait_ge(stored, 16 * NG)

    @block.gpsimd
    def _(pool):
        pool.tensor_copy(cw_st[:], cw_hl[:, 0:GT, :]).then_inc(cw_staged, 1)
        pool.memset(pick_f[:], 0.0).then_inc(pick_0, 1)
        pool.wait_ge(pick_0, 1)
        for i in range(2):
            pool.affine_select(out=pick_f[:], in_=pick_f[:], compare_op=ALU.not_equal, fill=1.0, base=-E * i,
                               pattern=[[-1, E]], channel_multiplier=1).then_inc(pick_1, 1)
            pool.wait_ge(pick_1, i + 1)
        with pool.Fori(1, NG) as g:
            pool.wait_ge(cw_turned, g)
            pool.tensor_copy(cw_st[:], cw_hl[:, bass.ds(g * GT, GT), :]).then_inc(cw_staged, 1)

    @block.scalar
    def _(act):
        def round_weights(e):
            if e % WB == 0:
                act.wait_ge(raw_loaded[e // WB], 16 * (2 * DC + 1))
            nc.scalar.activation(w_hi[:, e], w_raw[:, e], ACT.Copy).then_inc(w_rounded, 1)

        def root(g):
            act.wait_ge(ms_done, g + 1)
            nc.scalar.activation(ms[:], ms[:], ACT.Sqrt, scale=1.0 / NORM_G, bias=rms_eps[:]).then_inc(rms_done, 1)

        def round_output(g, ps):
            act.wait_ge(o_turned, g + 1)
            nc.scalar.activation(oT_hi[:], ps, ACT.Copy).then_inc(oT_rounded, 1)

        def copy_routing(g):
            act.wait_ge(cw_turned, g + 1)
            nc.scalar.activation(cwT[:], ps_c[0:2 * E, 0, :], ACT.Copy).then_inc(cwT_done, 1)

        def expert(g, e, first):
            s = g * NX + e
            act.wait_ge(h_ready, s + 1)
            nc.scalar.activation(act_h[:, e % 2, :], ps_h[e % 2][:, 0, :], ACT.Silu).then_inc(silu_done, 1)
            act.wait_ge(hid_done, s + 1)
            if not (first and e < 2):
                act.wait_ge(y_part, s - 1)
            nc.scalar.activation(hid_hi[:, e % 2, :], hid[:, e % 2, :], ACT.Copy).then_inc(hi_done, 1)

        def group(g, first=False, last=False):
            for e in range(NX):
                expert(g, e, first)
                if first and e + 2 < NX:
                    round_weights(e + 2)
                if first and e == 1:
                    round_output(0, ps_y[:].rearrange("p t d -> p (t d)"))
                if not last:
                    if e == AT_ROOT:
                        root(g + 1)
                    if e == AT_TURN_O:
                        round_output(g + 1, ps_c[:].rearrange("p c t -> p (c t)"))
                    if e == AT_TURN_CW:
                        copy_routing(g + 1)

        round_weights(0)
        act.wait_ge(pick_1, 2)
        nc.scalar.activation(pick[:], pick_f[:], ACT.Copy).then_inc(pick_2, 1)
        copy_routing(0)
        round_weights(1)
        root(0)
        act.wait_ge(wo_loaded, 16)
        nc.scalar.activation(wo_hi[:], wo_raw, ACT.Copy).then_inc(wo_rounded, 1)
        group(0, first=True)
        with act.Fori(0, PAIRS) as trip:
            for i in range(1, 3):
                group(trip * 2 + i)
        group(NG - 1, last=True)

    @block.vector
    def _(dve):
        def split_weights(e):
            dve.wait_ge(w_rounded, e + 1)
            nc.vector.tensor_tensor(w_lo[:, e], w_raw[:, e], w_hi[:, e].bitcast(F32), ALU.subtract
                                    ).then_inc(w_split, 1)

        def square(g):
            dve.wait_ge(o_loaded, 16 * (g + 1))
            wait(dve, o_turned, g)
            nc.vector.tensor_tensor(on[:], o_in[:], o_in[:], ALU.mult).then_inc(sq_done, 1)

        def sum_squares(g):
            dve.wait_ge(sq_done, g + 1)
            wait(dve, on_done, g)
            nc.vector.tensor_reduce(ms[:], on[:].rearrange("p t (n k) -> p t n k", k=NORM_G), AX_X, ALU.add
                                    ).then_inc(ms_done, 1)

        def scale(g):
            dve.wait_ge(rms_done, g + 1)
            nc.vector.reciprocal(ms[:], ms[:]).then_inc(rr_done, 1)
            dve.wait_ge(rr_done, g + 1)
            nc.vector.scalar_tensor_tensor(
                out=on[:].rearrange("p t (n k) -> p (t n) k", k=NORM_G),
                in0=o_in[:].rearrange("p t (n k) -> p (t n) k", k=NORM_G), scalar=1.0 - L_INIT,
                in1=ms[:].rearrange("p t n -> p (t n)").unsqueeze(2).broadcast_to([P, GT * D // NORM_G, NORM_G]),
                op0=ALU.mult, op1=ALU.mult).then_inc(on_done, 1)

        def split_output(g, ps):
            dve.wait_ge(oT_rounded, g + 1)
            nc.vector.tensor_tensor(oT_lo[:].rearrange("p c t -> p (c t)"), ps,
                                    oT_hi[:].rearrange("p c t -> p (c t)").bitcast(F32), ALU.subtract
                                    ).then_inc(oT_split, 1)

        def expert(g, e, first):
            s = g * NX + e
            later = not (first and e < 2)
            dve.wait_ge(silu_done, s + 1)
            if later:
                dve.wait_ge(hid_done, s - 1)
            nc.vector.tensor_tensor(mid[:, e % 2, :], ps_h[e % 2][:, 1, :], act_h[:, e % 2, :], ALU.mult
                                    ).then_inc(mid_done, 1)
            dve.wait_ge(mid_done, s + 1)
            if later:
                dve.wait_ge(lo_done, s - 1)
            if e < E:
                dve.wait_ge(c_ready, g * E + e + 1)
                nc.vector.tensor_tensor(hid[:, e % 2, :], ps_c[:, e % 2, :], mid[:, e % 2, :], ALU.mult
                                        ).then_inc(hid_done, 1)
            else:
                nc.vector.tensor_scalar(hid[:, e % 2, :], mid[:, e % 2, :], 1.0 / (TOP_K + 1.0), None, ALU.mult
                                        ).then_inc(hid_done, 1)
            dve.wait_ge(hi_done, s + 1)
            nc.vector.tensor_tensor(hid_lo[:, e % 2, :], hid[:, e % 2, :], hid_hi[:, e % 2, :].bitcast(F32),
                                    ALU.subtract).then_inc(lo_done, 1)

        def residual(g):
            dve.wait_ge(x_loaded, 16 * (g + 1))
            dve.wait_ge(y_part, NX * (g + 1))
            nc.vector.tensor_tensor(res[:], ps_y[:], res[:], ALU.add).then_inc(res_done, 1)

        def group(g, first=False, last=False):
            for e in range(NX):
                expert(g, e, first)
                if first and e + 2 < NX:
                    split_weights(e + 2)
                if first and e == 1:
                    split_output(0, ps_y[:].rearrange("p t d -> p (t d)"))
                if e == 0 and not first:
                    residual(g - 1)
                if not last:
                    if e == AT_SQUARE:
                        square(g + 1)
                    if e == AT_SUM:
                        sum_squares(g + 1)
                    if e == AT_SCALE:
                        scale(g + 1)
                    if e == AT_TURN_O:
                        split_output(g + 1, ps_c[:].rearrange("p c t -> p (c t)"))

        split_weights(0)
        square(0)
        sum_squares(0)
        split_weights(1)
        scale(0)
        dve.wait_ge(wo_rounded, 1)
        nc.vector.tensor_tensor(wo_lo, wo_raw, wo_hi[:].bitcast(F32), ALU.subtract).then_inc(wo_split, 1)
        group(0, first=True)
        with dve.Fori(0, PAIRS) as trip:
            for i in range(1, 3):
                group(trip * 2 + i)
        group(NG - 1, last=True)
        residual(NG - 1)

    @block.tensor
    def _(pe):
        def turn_routing(g):
            pe.wait_ge(cw_staged, g + 1)
            if not (isinstance(g, int) and g == 0):
                pe.wait_ge(oT_split, g + 1)
            for t in range(GT):
                last = nc.tensor.transpose(ps_c[0:2 * E, 0, t * P:(t + 1) * P], cw_st[:, t, :], ident[:])
            last.then_inc(cw_turned, 1)

        def turn_output(g, ps):
            pe.wait_ge(on_done, g + 1)
            if not (isinstance(g, int) and g == 0):
                pe.wait_ge(hid_done, (g - 1) * NX + E)
            for c in range(DC):
                for t in range(GT):
                    at = c * GRP + t * P
                    last = nc.tensor.transpose(ps[:, at:at + P], on[:, t, c * P:(c + 1) * P], ident[:])
            last.then_inc(o_turned, 1)

        def hidden(g, p, e, first):
            s = g * NX + e
            if e == 0:
                pe.wait_ge(xg_loaded, 16 * (g + 1))
            if first:
                pe.wait_ge(w_split, e + 1)
            if not (first and e < 2):
                pe.wait_ge(mid_done, s - 1)
            for i in range(2):
                k = 0
                for c in range(DC):
                    at = (i * DC + c) * H
                    for w, a in ((w_hi, 0), (w_lo, 0), (w_hi, 1)):
                        k += 1
                        last = nc.tensor.matmul(ps_h[e % 2][:, i, :], w[:, e, at:at + H], xg[:, p, a, c, :],
                                                start=(k == 1), stop=(k == 3 * DC))
            last.then_inc(h_ready, 1)

        def spread_routing(g, e):
            if e == 0 and isinstance(g, int) and g == 0:
                pe.wait_ge(pick_2, 1)
            if e == 0:
                pe.wait_ge(cwT_done, g + 1)
            if e >= 2:
                pe.wait_ge(hid_done, g * NX + e - 1)
            nc.tensor.matmul(ps_c[:, e % 2, :], pick[:, e:e + 1].broadcast_to([2 * E, P]), cwT[:], start=True,
                             stop=True).then_inc(c_ready, 1)

        def out_product(g, e):
            pe.wait_ge(lo_done, g * NX + e + 1)
            for t in range(GT):
                rows = slice(t * P, (t + 1) * P)
                for a, w in ((hid_hi, w_hi), (hid_hi, w_lo), (hid_lo, w_hi)):
                    last = nc.tensor.matmul(ps_y[:, t, :], a[:, e % 2, rows], w[:, e, 2 * DC * H:WCOL], start=False,
                                            stop=(e == NX - 1), skip_group_check=True)
            last.then_inc(y_part, 1)

        def attention_product(g):
            pe.wait_ge(oT_split, g + 1)
            if isinstance(g, int) and g == 0:
                pe.wait_ge(wo_split, 1)
            else:
                pe.wait_ge(res_done, g)
            for t in range(GT):
                rows = slice(t * P, (t + 1) * P)
                for c in range(DC):
                    for i, (a, w) in enumerate(((oT_hi, wo_hi), (oT_hi, wo_lo), (oT_lo, wo_hi))):
                        nc.tensor.matmul(ps_y[:, t, :], a[:, c, rows], w[:, c, :],
                                         start=(t % 2 == 0 and c == 0 and i == 0), stop=False, skip_group_check=True)

        def group(g, p, first=False, last=False):
            for e in range(NX):
                hidden(g, p, e, first)
                if e == 2:
                    attention_product(g)
                if e >= 2:
                    out_product(g, e - 2)
                elif not first:
                    out_product(g - 1, NX - 2 + e)
                if first and e == 0:
                    turn_routing(0)
                if e < E:
                    spread_routing(g, e)
                if first and e == 1:
                    turn_output(0, ps_y[:].rearrange("p t d -> p (t d)"))
                if not last:
                    if e == AT_TURN_O:
                        turn_output(g + 1, ps_c[:].rearrange("p c t -> p (c t)"))
                    if e == AT_TURN_CW:
                        turn_routing(g + 1)

        group(0, 0, first=True)
        with pe.Fori(0, PAIRS) as trip:
            for i in range(1, 3):
                group(trip * 2 + i, i % 2)
        group(NG - 1, 1, last=True)
        for e in range(NX - 2, NX):
            out_product(NG - 1, e)


_INS = ["L0_attn_x", "L0_attn_l_q1", "L0_attn_l_k1", "L0_attn_l_q2", "L0_attn_l_k2", "L0_attn_wqk",
        "L0_attn_wv", "L0_attn_wo", "L0_ffn_w_router", "L0_ffn_we1", "L0_ffn_we3", "L0_ffn_we2", "L0_ffn_ws1",
        "L0_ffn_ws3", "L0_ffn_ws2"]
_TURNED = {"L0_attn_wv", "L0_attn_wo"}


def kernel(**inputs):
    import numpy as _np
    import concourse.bacc as _bacc
    from concourse import mybir as _mybir
    from concourse.bass_utils import run_bass_kernel_spmd as _run

    nc = _bacc.Bacc("TRN2", target_bir_lowering=False, num_devices=1)
    arrays, args = {}, []
    wqk = _np.stack([_np.asarray(inputs["L0_attn_wq"]), _np.asarray(inputs["L0_attn_wk"])])
    wqk = wqk.reshape(2, 2, NH, DH, D).transpose(2, 4, 0, 1, 3).reshape(NH, D, 4 * DH)
    for name in _INS:
        a = wqk if name == "L0_attn_wqk" else _np.asarray(inputs[name])
        a = _np.ascontiguousarray(a.T if name in _TURNED else a)
        arrays[f"in_{name}"] = a
        args.append(nc.dram_tensor(f"in_{name}", a.shape, _mybir.dt.from_np(a.dtype), kind="ExternalInput").ap())
    out = nc.dram_tensor("out_0", (B, S, D), _mybir.dt.float32, kind="ExternalOutput").ap()
    o_dram = nc.dram_tensor("attention_out", (T, D), _mybir.dt.float32, kind="Internal").ap()
    xT_dram = nc.dram_tensor("tokens_turned", (NG, P, 2, DC, GRP), _mybir.dt.float32, kind="Internal").ap()
    build(nc, *args, out, o_dram, xT_dram)
    r = _run(nc, [arrays], core_ids=[0])
    return r.results[0]["out_0"]
```
